# Optimizing a Trainium2 kernel written in Bass

```python
import numpy as np
import jax
import jax.numpy as jnp

def _softmax(x, axis=-1):
    return jax.nn.softmax(x, axis=axis)

def _gelu(x):
    return jax.nn.gelu(x, approximate=True)

def _silu(x):
    return jax.nn.silu(x)

def _sigmoid(x):
    return jax.nn.sigmoid(x)

def _layernorm(x, axis=-1, eps=1e-05):
    m = jnp.mean(x, axis=axis, keepdims=True)
    v = jnp.var(x, axis=axis, keepdims=True)
    return (x - m) / jnp.sqrt(v + eps)

def _scatter_add(tgt, idx, src, axis=0):
    return tgt.at[idx].add(src)

def _segment_sum(src, seg, n):
    return jax.ops.segment_sum(src, seg, n)
kernel_name = 'mk_prb_d1_jaxref_r8_17d34e'

def setup_inputs(seed: int=0):
    np.random.seed(seed)
    _w = jnp.asarray

    def _L0_attn_setup():
        import jax, jax.numpy as jnp
        import numpy as np
        H, NS = (16, 8)
        key = jax.random.key(seed)
        ks = jax.random.split(key, 8)
        B, S, Dm = (1, 256, 256)
        hd = Dm // H
        return {'hidden_states': jax.random.normal(ks[0], (B, S, Dm), jnp.float32), 'Wq': jax.random.normal(ks[1], (Dm, Dm), jnp.float32) * 0.02, 'Wk': jax.random.normal(ks[2], (Dm, Dm), jnp.float32) * 0.02, 'Wv': jax.random.normal(ks[3], (Dm, Dm), jnp.float32) * 0.02, 'Wo': jax.random.normal(ks[4], (Dm, Dm), jnp.float32) * 0.02, 'splat_positions': jax.random.normal(ks[5], (H, NS, hd), jnp.float32) * 0.02, 'splat_directions': jax.random.normal(ks[6], (H, NS, hd), jnp.float32) * 0.02, 'splat_log_scales': jnp.full((H, NS), np.float32(np.log(0.8)), jnp.float32), 'splat_log_amplitudes': jnp.full((H, NS), np.float32(-np.log(NS)), jnp.float32), 'directional_strength': jnp.float32(0.4), 'position_sensitivity': jnp.float32(0.3), 'gsa_strength': jnp.float32(-4.0)}
    _L0_attn_in = _L0_attn_setup()

    def _L0_ffn_setup():
        import jax, jax.numpy as jnp
        import numpy as np
        E = 16
        K = 2
        D = 256
        I = 176
        CAP = 128
        VOCAB = 16160
        key = jax.random.key(seed)
        ks = jax.random.split(key, 11)
        B, S = (4, 128)
        sd = 1.0 / np.sqrt(D)
        si = 1.0 / np.sqrt(I)
        return {'x': jax.random.normal(ks[0], (B, S, D), jnp.float32), 'input_ids': jax.random.randint(ks[1], (B, S), 0, VOCAB, dtype=jnp.int64), 'gate_w': jax.random.normal(ks[2], (E, D), jnp.float32) * sd, 'gate_b': jax.random.normal(ks[3], (E,), jnp.float32) * 0.01, 'W1': jax.random.normal(ks[4], (E, I, D), jnp.float32) * sd, 'W3': jax.random.normal(ks[5], (E, I, D), jnp.float32) * sd, 'W2': jax.random.normal(ks[6], (E, D, I), jnp.float32) * si, 'Ws1': jax.random.normal(ks[7], (I, D), jnp.float32) * sd, 'Ws3': jax.random.normal(ks[8], (I, D), jnp.float32) * sd, 'Ws2': jax.random.normal(ks[9], (D, I), jnp.float32) * si}
    _L0_ffn_in = _L0_ffn_setup()
    _d = {'L0_attn_hidden_states': _L0_attn_in['hidden_states'], 'L0_attn_Wq': _L0_attn_in['Wq'], 'L0_attn_Wk': _L0_attn_in['Wk'], 'L0_attn_Wv': _L0_attn_in['Wv'], 'L0_attn_Wo': _L0_attn_in['Wo'], 'L0_attn_splat_positions': _L0_attn_in['splat_positions'], 'L0_attn_splat_directions': _L0_attn_in['splat_directions'], 'L0_attn_splat_log_scales': _L0_attn_in['splat_log_scales'], 'L0_attn_splat_log_amplitudes': _L0_attn_in['splat_log_amplitudes'], 'L0_attn_directional_strength': _L0_attn_in['directional_strength'], 'L0_attn_position_sensitivity': _L0_attn_in['position_sensitivity'], 'L0_attn_gsa_strength': _L0_attn_in['gsa_strength'], 'L0_ffn_input_ids': _L0_ffn_in['input_ids'], 'L0_ffn_gate_w': _L0_ffn_in['gate_w'], 'L0_ffn_gate_b': _L0_ffn_in['gate_b'], 'L0_ffn_W1': _L0_ffn_in['W1'], 'L0_ffn_W3': _L0_ffn_in['W3'], 'L0_ffn_W2': _L0_ffn_in['W2'], 'L0_ffn_Ws1': _L0_ffn_in['Ws1'], 'L0_ffn_Ws3': _L0_ffn_in['Ws3'], 'L0_ffn_Ws2': _L0_ffn_in['Ws2']}
    _x0 = _d['L0_attn_hidden_states']
    _d['L0_attn_hidden_states'] = jax.random.normal(jax.random.fold_in(jax.random.key(seed), 1), (1, 1024, 256), dtype=_x0.dtype)
    del _x0
    return _d

def reference(L0_attn_hidden_states, L0_attn_Wq, L0_attn_Wk, L0_attn_Wv, L0_attn_Wo, L0_attn_splat_positions, L0_attn_splat_directions, L0_attn_splat_log_scales, L0_attn_splat_log_amplitudes, L0_attn_directional_strength, L0_attn_position_sensitivity, L0_attn_gsa_strength, L0_ffn_input_ids, L0_ffn_gate_w, L0_ffn_gate_b, L0_ffn_W1, L0_ffn_W3, L0_ffn_W2, L0_ffn_Ws1, L0_ffn_Ws3, L0_ffn_Ws2):

    def _L0_attn_ref(hidden_states, Wq, Wk, Wv, Wo, splat_positions, splat_directions, splat_log_scales, splat_log_amplitudes, directional_strength, position_sensitivity, gsa_strength):
        import jax, jax.numpy as jnp
        import numpy as np
        H, NS = (16, 8)
        B, S, Dm = hidden_states.shape
        Hn, Ns, hd = splat_positions.shape

        def heads(x):
            return x.reshape(B, S, Hn, hd).transpose(0, 2, 1, 3)
        q = heads(hidden_states @ Wq.T)
        k = heads(hidden_states @ Wk.T)
        v = heads(hidden_states @ Wv.T)
        scores = jnp.einsum('bhid,bhjd->bhij', q, k) / jnp.sqrt(jnp.float32(hd))
        mask = jnp.tril(jnp.ones((S, S), bool))
        neg = jnp.finfo(scores.dtype).min

        def out_proj(attn):
            o = jnp.einsum('bhij,bhjd->bhid', attn, v)
            return o.transpose(0, 2, 1, 3).reshape(B, S, Dm) @ Wo.T
        std_out = out_proj(jax.nn.softmax(jnp.where(mask, scores, neg), axis=-1))
        scales = jnp.exp(splat_log_scales)
        amps = jnp.exp(splat_log_amplitudes)
        dirn = splat_directions / (jnp.linalg.norm(splat_directions, axis=-1, keepdims=True) + 1e-08)

        def splat_feats(x):
            diff = x[:, :, :, None, :] - splat_positions[None, :, None, :, :]
            gauss = jnp.exp(-0.5 * jnp.sum(diff * diff, -1) / (scales ** 2)[None, :, None, :])
            dirp = jnp.tanh(jnp.einsum('bhsnd,hnd->bhsn', diff, dirn))
            return (gauss, dirp)
        qg, qd = splat_feats(q)
        kg, kd = splat_feats(k)
        amp_b = amps[None, :, None, :]
        splat_attn = jnp.einsum('bhin,bhjn->bhij', amp_b * qg, kg) + directional_strength * jnp.einsum('bhin,bhjn->bhij', amp_b * qg * qd, kg * kd)
        gsa_scores = scores + position_sensitivity * splat_attn
        gsa_out = out_proj(jax.nn.softmax(jnp.where(mask, gsa_scores, neg), axis=-1))
        blend = jnp.minimum(jnp.float32(0.03), jax.nn.sigmoid(gsa_strength) * 0.15)
        return (1.0 - blend) * std_out + blend * gsa_out

    def _L0_ffn_ref(x, input_ids, gate_w, gate_b, W1, W3, W2, Ws1, Ws3, Ws2):
        import jax, jax.numpy as jnp
        import numpy as np
        E = 16
        K = 2
        D = 256
        I = 176
        CAP = 128
        VOCAB = 16160
        shape = x.shape
        xt = x.reshape(-1, D)
        T = xt.shape[0]
        logits = xt.astype(jnp.float32) @ gate_w.astype(jnp.float32).T
        scores = jnp.sqrt(jax.nn.softplus(logits))
        _, idx = jax.lax.top_k(scores + gate_b, K)
        w = jnp.take_along_axis(scores, idx, axis=1)
        w = w / jnp.sum(w, axis=1, keepdims=True)
        e = idx.reshape(-1)
        onehot = jax.nn.one_hot(e, E, dtype=jnp.int32)
        pos = jnp.sum(onehot * (jnp.cumsum(onehot, axis=0) - 1), axis=1)
        valid = pos < CAP
        posc = jnp.where(valid, pos, 0)
        x_pairs = jnp.repeat(xt, K, axis=0)
        x_pairs = jnp.where(valid[:, None], x_pairs, 0.0)
        buf = jnp.zeros((E, CAP, D), xt.dtype).at[e, posc].add(x_pairs)
        g = jnp.einsum('ecd,eid->eci', buf, W1).astype(jnp.float32)
        u = jnp.einsum('ecd,eid->eci', buf, W3).astype(jnp.float32)
        h = (jax.nn.silu(g) * u).astype(xt.dtype)
        out = jnp.einsum('eci,edi->ecd', h, W2)
        y_pairs = out[e, posc] * (w.reshape(-1) * valid)[:, None]
        y = y_pairs.reshape(T, K, D).sum(axis=1)
        gs = jax.nn.silu((xt @ Ws1.T).astype(jnp.float32))
        us = (xt @ Ws3.T).astype(jnp.float32)
        shared = (gs * us).astype(xt.dtype) @ Ws2.T
        return (y + shared).astype(x.dtype).reshape(shape)
    x = L0_attn_hidden_states
    xn = _layernorm(x, axis=-1)
    x = x + _L0_attn_ref(xn, L0_attn_Wq, L0_attn_Wk, L0_attn_Wv, L0_attn_Wo, L0_attn_splat_positions, L0_attn_splat_directions, L0_attn_splat_log_scales, L0_attn_splat_log_amplitudes, L0_attn_directional_strength, L0_attn_position_sensitivity, L0_attn_gsa_strength) + _L0_ffn_ref(xn, L0_ffn_input_ids, L0_ffn_gate_w, L0_ffn_gate_b, L0_ffn_W1, L0_ffn_W3, L0_ffn_W2, L0_ffn_Ws1, L0_ffn_Ws3, L0_ffn_Ws2)
    return x

_drawn_inputs = setup_inputs


def setup_inputs(seed=0):
    import zlib

    import numpy as np

    out = dict(_drawn_inputs(seed))
    spreads = {'L0_attn_splat_log_scales': (-0.2231435477733612, 0.6),
     'L0_attn_splat_log_amplitudes': (-2.079441547393799, 0.6)}
    factors = {'L0_attn_Wq': 8.0,
     'L0_attn_Wk': 8.0,
     'L0_attn_Wv': 7.865,
     'L0_attn_Wo': 8.0,
     'L0_attn_splat_positions': 8.0,
     'L0_attn_splat_directions': 8.0,
     'L0_ffn_gate_b': 2.842}
    for name, (base, spread) in spreads.items():
        noise = np.random.default_rng([zlib.crc32(name.encode()), seed]).standard_normal(out[name].shape)
        drawn = base * np.exp(spread * noise) if base else spread * noise
        out[name] = jnp.asarray(drawn.astype(out[name].dtype))
    for name, factor in factors.items():
        out[name] = (out[name] * factor).astype(out[name].dtype)
    return out
```

```python
from contextlib import ExitStack

import concourse.bass as bass
from concourse import mybir


def bass_splat_attention_moe_layer(nc, x, wqkvo, positions, directions, log_scales, log_amplitudes,
                                   strength, sensitivity, gsa_gate, gate_w, gate_b,
                                   w13, w2, ws13, ws2, out):
    f32, bf16, u32 = mybir.dt.float32, mybir.dt.bfloat16, mybir.dt.uint32
    ALU, ACT, AX = mybir.AluOpType, mybir.ActivationFunctionType, mybir.AxisListType

    T, D = x.shape
    P = 128
    NT = T // P
    KD = D // P
    H, NS, HD = 16, 8, 16
    E, I, CAP = 16, 176, 128
    I2 = I // 2
    CH = 512
    NC = T // CH
    TC = CH // P
    GH = 2
    NG = H // GH
    EG = E // NG
    NF = EG + 1
    SPL = 3
    RUNS = [(0, 0, 3, 0), (3, 0, 2, 1), (5, 0, 1, 2)]
    KR = HD * 6
    KS = KR + 2
    NEG = -1.0e30
    DUMP = E * CAP
    EPS = 1e-5

    xn_d = nc.dram_tensor("xn_scratch", (T, D), f32).ap()
    ids_d = nc.dram_tensor("ids_scratch", (DUMP + 2 * T, 1), u32).ap()
    ye_d = nc.dram_tensor("ye_scratch", (E * CAP, D), f32).ap()
    parts_d = [nc.dram_tensor(f"parts_scratch{n}", (H, SPL, HD, T), bf16).ap() for n in range(4)]

    ctx = ExitStack()
    with ctx:
        def sb(name, shape, dt):
            return ctx.enter_context(nc.sbuf_tensor(name, shape, dt))

        def sem(name):
            return ctx.enter_context(nc.semaphore(name))

        acc = sb("acc", [P, NT, D], f32)
        xn = sb("xn", [P, NT, D], f32)
        xnT = sb("xnT", [P, KD, T], f32)
        wt = sb("wt", [P, 4, KD, D], f32)
        v_all = sb("v_all", [P, NT, D], f32)
        v_st = sb("v_st", [P, 2, NT, GH, 2 * HD], f32)
        stage = [sb(f"stage{n}", [KS, 2, GH, T], bf16) for n in range(4)]
        qs, ks, fq, fk = stage
        arena_p = sb("arena_p", [P, 4, 1024], f32)
        arena_o = sb("arena_o", [P, 4, T], f32)
        rest_ = sb("rest", [P, 2, T], f32)
        split = sb("split", [P, 4, SPL, 2, T], bf16)
        sq = split[:, 2:4, :, :, :].rearrange("p a b c t -> p (a b c t)").bitcast(f32)[:, 0:2 * KD * T] \
            .rearrange("p (s m t) -> p s m t", s=2, m=KD)
        qkT = arena_p[:, :, :].rearrange("p (s m) t -> p s m t", s=2)
        feat = arena_o[:, :, :].rearrange("p (s m) t -> p s m t", s=2)
        probs = arena_p[:, :, :].rearrange("p (v s) (h n) -> p v s h n", v=2, h=GH)
        o_nat = arena_o[:, 0:2, :].rearrange("p a t -> p (a t)").rearrange("p (n d) -> p n d", d=D)
        oT = arena_o[:, 2:4, :]
        gath = split[:, 0:2, :, :, :].rearrange("p a b c t -> p (a b c t)")[:, 0:2 * 2 * D * 2].bitcast(f32) \
            .rearrange("p (k n d) -> p k n d", k=2, n=2)

        w13_sb = sb("w13_sb", [P, NF, KD, 2 * I], f32)
        w2_sb = sb("w2_sb", [I2, NF, 2, D], f32)
        xs = sb("xs", [P, D], f32)
        xe = sb("xe", [P, EG, D], f32)
        xeT = sb("xeT", [P, KD, P], f32)
        th = sb("th", [P, I], f32)
        h1 = sb("h1", [P, I], f32)
        hh = sb("hh", [P, I], f32)
        hT = sb("hT", [I2, 2, P], f32)
        ye = sb("ye", [P, EG, D], f32)
        pv_sb = sb("pv_sb", [P, CH], f32)
        rec = sb("rec", [P, TC, 4], f32)
        recw = sb("recw", [P, TC, 4], f32)
        onv = sb("onv", [P, TC, 4, HD], f32)
        mx = sb("mx", [P, 2, GH, TC, 2], f32)
        mneg = sb("mneg", [P, 2, GH, TC], f32)
        mhl = sb("mhl", [P, 2, 2, GH * TC], bf16)
        mT = sb("mT", [2 * GH * TC, 2, P], bf16)

        ident = sb("ident", [P, P], f32)
        ident_b = sb("ident_b", [P, P], bf16)
        mask_t = sb("mask_t", [P, P], bf16)
        mask_n = sb("mask_n", [P, P], bf16)
        upper = sb("upper", [P, P], bf16)
        ones_b = sb("ones_b", [P, P], bf16)
        blockm = sb("blockm", [P, NS, HD], f32)
        iota_r = sb("iota_r", [P, NT, E], f32)
        iota_s = sb("iota_s", [P, NT, E], f32)
        iota_i = sb("iota_i", [P, 2, NT], u32)
        tok = sb("tok", [P, NT], u32)
        dump = sb("dump", [P, 2, NT], f32)
        zero_i = sb("zero_i", [E, CAP], u32)

        pos = sb("pos", [P, HD], f32)
        dire = sb("dire", [P, HD], f32)
        par = sb("par", [P, 24], f32)
        (LS, LA, PS, DS, GG, IS2, AMP, NSQ, NRM, RN, PD, PP, BG, C1, C2, BD, HI2, EG_, B_, B1_, TMP, TMP2) = \
            [par[:, n:n + 1] for n in range(22)]
        tmp16 = sb("tmp16", [P, 4, HD], f32)
        gwide = sb("gwide", [P, 3, P], f32)
        gT = sb("gT", [P, 3, P], f32)
        blendw = sb("blendw", [P, 4], f32)
        stats = sb("stats", [P, NT, 6], f32)
        mv = sb("mv", [P, NT, 2], f32)
        vstd = sb("vstd", [P, 2, NT], f32)
        gw_sb = sb("gw_sb", [P, KD, E], f32)
        gb_sb = sb("gb_sb", [P, 1, E], f32)
        g_ = [sb(f"g{n}", [P, NT, E], f32) for n in range(12)]
        ohs = sb("ohs", [P, NT, E], bf16)
        r_ = sb("r_", [P, 16, NT], f32)
        sidx = sb("sidx", [P, 2, NT], u32)
        gidx = sb("gidx", [P, 2, NT], u32)
        pairw = sb("pairw", [P, 2, NT], f32)
        ids_sb = sb("ids_sb", [P, E], u32)
        ids_cur = sb("ids_cur", [P, EG, 1], u32)

        ps = ctx.enter_context(nc.psum_tensor("ps", [P, 8, CH], f32))
        psb = ps[:, :, :].rearrange("p b n -> p (b n)").bitcast(bf16).rearrange("p (b n) -> p b n", b=8)

        par_in, wqk_in, wvo_in, gate_in, ws_in = (sem(n) for n in ("par_in", "wqk_in", "wvo_in", "gate_in", "ws_in"))
        consts = sem("consts")
        dve_step, pool_step = sem("dve_step"), sem("pool_step")
        x_in = [sem(f"x_in{n}") for n in range(NC)]
        pool_ids = sem("pool_ids")
        norm_ready, norm_root, var_ready, var_root = sem("norm_ready"), sem("norm_root"), sem("var_ready"), sem("var_root")
        xn_ready, par_exp, gw_ready, gT_ready, gate_dve, gate_act = (sem(n) for n in ("xn_ready", "par_exp", "gw_ready", "gT_ready", "gate_dve", "gate_act"))
        ohs_ready, slots_ready, v_done = sem("ohs_ready"), sem("slots_ready"), sem("v_done")
        first_part, squares, features, parts_ready = sem("first_part"), sem("squares"), sem("features"), sem("parts_ready")
        pro_full = sem("pro_full")
        xn_out, ids0_out, ids_out, ids_in = sem("xn_out"), sem("ids0_out"), sem("ids_out"), sem("ids_in")
        parts_out = [sem(f"parts_out{n}") for n in range(8)]
        qk_in = [sem(f"qk_in{n}") for n in range(2)]
        f_in = [sem(f"f_in{n}") for n in range(2)]
        aux_full, aux_free = sem("aux_full"), sem("aux_free")
        std_ready, std_exp, gsa_ready, gsa_exp = sem("std_ready"), sem("std_exp"), sem("gsa_ready"), sem("gsa_exp")
        acc_full, acc_free, pv_copied = sem("acc_full"), sem("acc_free"), sem("pv_copied")
        shift_ready = sem("shift_ready")
        shift_in = [sem(f"shift_in{n}") for n in range(NC)]
        v_ready, mhl_ready, xs_ready, o_ready = sem("v_ready"), sem("mhl_ready"), sem("xs_ready"), sem("o_ready")
        xe_in = [sem(f"xe_in{n}") for n in range(EG)]
        w_in = [sem(f"w_in{n}") for n in range(EG)]
        xT_ready, th_ready, h_ready, hT_ready, ye_ready = (sem(n) for n in ("xT_ready", "th_ready", "h_ready", "hT_ready", "ye_ready"))
        ye_out = [sem(f"ye_out{n}") for n in range(EG)]
        gath_in = [sem(f"gath_in{n}") for n in range(2)]
        gath_used = sem("gath_used")
        oT_full, oT_ready, y_full, y_done, y_out = (sem(n) for n in ("oT_full", "oT_ready", "y_full", "y_done", "y_out"))

        block = ctx.enter_context(nc.Block())

        PRO = [("xnT", (k, tq)) for tq in range(NC) for k in range(KD)] + [("par", 0), ("gate", 0)]
        PRO += [("proj", (s, m, tc)) for m in range(KD) for s in range(2) for tc in range(NC)]
        PRO += [("feat", (s, tc, w)) for s in range(2) for tc in range(NC) for w in range(2)]
        PRO += [("cum", 0)] + [("v", n) for n in range(NT // 2)]
        READER = {"xnT": "act", "par": "dve", "gate": "dve", "proj": "act", "feat": "act", "cum": "dve", "v": "act"}
        PB = 6
        pro_act, pro_dve = sem("pro_act"), sem("pro_dve")
        reads = []
        for n, (kind, _) in enumerate(PRO):
            who = READER[kind]
            reads.append((pro_act if who == "act" else pro_dve, 1 + sum(READER[k] == who for k, _ in PRO[:n])))

        PAIRS = [(ic, 2 * p) for ic in range(NC) for p in range((ic + 1) * TC // 2)]
        NP = len(PAIRS)
        max0 = [("max", (h, it, 0)) for h in range(GH) for it in range(TC)]
        max1 = [("max", (h, it, pc)) for h in range(GH) for it in range(TC, NT) for pc in range(2)]
        AUX = [[] for _ in range(NP + 1)]

        def ffn(a, f):
            return [(a, f)]
        AUX[0] = ffn("xT", 0) + ffn("gu", 0)
        AUX[1] = ffn("hT", 0) + ffn("xT", 1) + ffn("y", 0) + ffn("gu", 1)
        AUX[2] = max0[0:2] + ffn("hT", 1) + max0[2:4] + ffn("y", 1) + [("oT", 0)] + max0[4:6]
        AUX[3] = max0[6:8] + ffn("xT", 2) + [("shift", 0)] + max1[0:2] + ffn("gu", 2) + max1[2:4]
        AUX[4] = max1[4:6] + ffn("hT", 2) + max1[6:8] + ffn("y", 2) + max1[8:10]
        AUX[5] = max1[10:14]
        AUX[6] = max1[14:16] + [("shift", 1), ("oT", 1)]
        FLAT = [t for a in AUX for t in a]
        NAUX = len(FLAT)
        assert NAUX % 2 == 0
        LAST = [[t for t in a if t[0] not in ("max", "shift")] for a in AUX]
        PRE = max0 + [("shift", 0)] + max1 + [("shift", 1)]
        NPRE = len(PRE)
        assert NPRE % 2 == 0

        FLAT_LAST = [t for a in LAST for t in a]

        def aux_index(task):
            return NPRE + FLAT.index(task)

        def aux_bank(g, task, last):
            plan = PRE if isinstance(g, int) and g < 0 else FLAT_LAST if last else FLAT
            return 6 + plan.index(task) % 2

        def aux_count(g, task, last):
            if isinstance(g, int) and g < 0:
                return 1 + PRE.index(task)
            if last:
                return NPRE + NAUX * (NG - 1) + FLAT_LAST.index(task) + 1
            return g * NAUX + (aux_index(task) + 1)

        SPLIT_ORDER = [(0, 0), (1, 0), (2, 0), (2, 1), (3, 0), (3, 1), (0, 1), (1, 1)]

        def shape_of(ic, jb):
            off = max(0, jb * P - ic * CH)
            return off, jb // TC == ic

        @block.gpsimd
        def _(pool):
            steps = [0]

            def link(ins):
                steps[0] += 1
                ins.then_inc(pool_step, 1)
                pool.wait_ge(pool_step, steps[0])

            def select(t, op, fill, base, pattern, mult):
                return nc.gpsimd.affine_select(out=t, in_=t, compare_op=op, fill=fill, base=base,
                                               pattern=pattern, channel_multiplier=mult)
            nc.gpsimd.memset(ident[:, :], 0.0)
            nc.gpsimd.memset(ident_b[:, :], 0.0)
            nc.gpsimd.memset(mask_t[:, :], 0.0)
            nc.gpsimd.memset(mask_n[:, :], 0.0)
            nc.gpsimd.memset(upper[:, :], 1.0)
            nc.gpsimd.memset(ones_b[:, :], 1.0)
            nc.gpsimd.memset(zero_i[:, :], 0)
            link(nc.gpsimd.memset(blockm[:, :, :], 1.0))
            select(ident[:, :], ALU.not_equal, 1.0, 0, [[-1, P]], 1)
            select(ident_b[:, :], ALU.not_equal, 1.0, 0, [[-1, P]], 1)
            select(mask_t[:, :], ALU.is_ge, NEG, 0, [[1, P]], -1)
            select(mask_n[:, :], ALU.is_ge, NEG, 0, [[-1, P]], 1)
            link(select(upper[:, :], ALU.is_gt, 0.0, 0, [[1, P]], -1))
            for half in range(2):
                rows = blockm[64 * half:64 * half + 64, :, :]
                link(select(rows, ALU.is_ge, 0.0, 0, [[-NS, 8], [0, HD]], 1))
            nc.gpsimd.iota(iota_i[:, :, :], [[T, 2], [P, NT]], base=DUMP, channel_multiplier=1)
            nc.gpsimd.iota(tok[:, :], [[P, NT]], base=0, channel_multiplier=1)
            nc.gpsimd.iota(iota_r[:, :, :], [[0, NT], [-1, E]], base=E, channel_multiplier=0,
                           allow_small_or_imprecise_dtypes=True)
            link(nc.gpsimd.iota(iota_s[:, :, :], [[0, NT], [CAP, E]], base=0, channel_multiplier=0,
                                allow_small_or_imprecise_dtypes=True))
            for half in range(2):
                rows = blockm[64 * half:64 * half + 64, :, :]
                link(select(rows, ALU.is_ge, 0.0, NS - 1, [[NS, 8], [0, HD]], -1))
            link(nc.gpsimd.tensor_copy(dump[:, :, :], iota_i[:, :, :]))
            for n in range(4):
                link(nc.gpsimd.memset(stage[n][KR:KS, :, :, :], float(n % 2)))
            nc.gpsimd.memset(v_st[:, :, :, :, HD:], 1.0).then_inc(consts, 1)

            pool.wait_ge(ids0_out, 16)
            pool.wait_ge(slots_ready, 2)
            for k in range(2):
                for n in range(NT):
                    nc.gpsimd.indirect_dma_start(
                        out=ids_d[:, :], out_offset=bass.IndirectOffsetOnAxis(ap=sidx[:, k, n:n + 1], axis=0),
                        in_=tok[:, n:n + 1], in_offset=None).then_inc(ids_out, 16)
            pool.wait_ge(ids_out, 16 * 2 * NT)
            with nc.allow_non_contiguous_dma(reason="2,048 ids"):
                pool.dma_start(ids_sb[:, :], ids_d[0:DUMP, :].rearrange("(e c) o -> c (e o)", c=CAP)).then_inc(ids_in, 16)
            pool.wait_ge(ids_in, 16)
            pool.wait_ge(xn_out, 16)

            def values(g):
                src = v_all[:, :, bass.ds(g * (GH * HD), GH * HD)].rearrange("p n (h d) -> p n h d", h=GH)
                dst = v_st[:, bass.ds(g % 2, 1), :, :, 0:HD].rearrange("p o n h d -> p (o n) h d")
                nc.gpsimd.tensor_copy(dst, src).then_inc(v_ready, 1)

            def gather(g, f, first):
                if not first:
                    pool.wait_ge(aux_full, (g - 1) * NAUX + aux_index(("xT", f)) + 1)
                    pool.wait_ge(xe_in[f], 16 * g)
                nc.gpsimd.tensor_copy(ids_cur[:, f, :], ids_sb[:, bass.ds(g * EG + f, 1)]).then_inc(pool_ids, 1)
                pool.wait_ge(pool_ids, g * EG + (f + 1))
                pool.nop(nofuse=True)
                nc.gpsimd.indirect_dma_start(
                    out=xe[:, f, :], out_offset=None, in_=xn_d[:, :],
                    in_offset=bass.IndirectOffsetOnAxis(ap=ids_cur[:, f, :], axis=0)).then_inc(xe_in[f], 16)

            for f in range(EG):
                gather(0, f, True)
            pool.wait_ge(v_done, NT // 2)
            values(0)
            values(1)
            with pool.Fori(1, NG - 1) as g:
                for f in range(EG):
                    gather(g, f, False)
                pool.wait_ge(acc_full, g * 2)
                values(g + 1)
            for f in range(EG):
                gather(NG - 1, f, False)

            for f in range(EG):
                pool.wait_ge(ye_out[f], 16 * NG)
            for n in range(NT):
                for k in range(2):
                    if n >= 2:
                        pool.wait_ge(gath_used, 2 * (n - 2) + k + 1)
                    nc.gpsimd.indirect_dma_start(
                        out=gath[:, k, n % 2, :], out_offset=None, in_=ye_d[:, :],
                        in_offset=bass.IndirectOffsetOnAxis(ap=gidx[:, k, n:n + 1], axis=0)).then_inc(gath_in[n % 2], 16)


        @block.sync
        def _(sp):
            for n in range(NC):
                sp.dma_start(acc[:, n * TC:(n + 1) * TC, :],
                             x[n * CH:(n + 1) * CH, :].rearrange("(n p) d -> p n d", p=P)).then_inc(x_in[n], 16)
            w_v = wqkvo.rearrange("w (k p) d -> p w k d", p=P)
            for w in range(2):
                sp.dma_start(wt[:, w, :, :], w_v[:, w, :, :]).then_inc(wqk_in, 16)
            for f in range(EG):
                sp.dma_start(w13_sb[:, f, :, :], w13[f, :, :].rearrange("(k p) i -> p k i", p=P)).then_inc(w_in[f], 16)
                sp.dma_start(w2_sb[:, f, :, :], w2[f, :, :].rearrange("(k p) d -> p k d", p=I2)).then_inc(w_in[f], 16)
            for w in range(2, 4):
                sp.dma_start(wt[:, w, :, :], w_v[:, w, :, :]).then_inc(wvo_in, 16)
            sp.dma_start(w13_sb[:, EG, :, :], ws13.rearrange("(k p) i -> p k i", p=P)).then_inc(ws_in, 16)
            sp.dma_start(w2_sb[:, EG, :, :], ws2.rearrange("(k p) d -> p k d", p=I2)).then_inc(ws_in, 16)
            sp.wait_ge(xn_ready, NT)
            sp.dma_start(xn_d.rearrange("(n p) d -> p n d", p=P), xn[:, :, :]).then_inc(xn_out, 16)
            for at, (n, m) in enumerate(SPLIT_ORDER):
                sp.wait_ge(parts_ready, at + 1)
                for s in range(SPL):
                    slot = s if n % 2 == 0 else SPL - 1 - s
                    if n < 2:
                        dst = parts_d[n][m * NS:(m + 1) * NS, slot, :, :]
                    else:
                        dst = parts_d[n][:, slot, m * NS:(m + 1) * NS, :]
                    sp.dma_start(dst, split[:, n, s, m, :]).then_inc(parts_out[at], 16)

            def load_stage(g, pr):
                for n in range(4):
                    for row, qp, num, kp in RUNS:
                        part = qp if n % 2 == 0 else kp
                        src = parts_d[n][bass.ds(g * GH, GH), part:part + num, :, :].rearrange("h s r t -> (s r) h t")
                        sp.dma_start(stage[n][row * HD:(row + num) * HD, pr, :, :], src)\
                          .then_inc(qk_in[pr] if n < 2 else f_in[pr], 16)

            def shift_rows(gm, ic, pr):
                sp.wait_ge(aux_free, aux_count(gm, ("shift", ic), False))
                for hl in range(2):
                    for h in range(GH):
                        row = (hl * GH + h) * TC
                        sp.dma_start(qs[KR + hl:KR + hl + 1, pr, h, ic * CH:(ic + 1) * CH],
                                     mT[row:row + TC, ic, :]).then_inc(shift_in[ic], 16)

            for at in range(6):
                sp.wait_ge(parts_out[at], 16 * SPL)
            load_stage(0, 0)
            for ic in range(NC):
                shift_rows(-1, ic, 0)
            for at in range(6, 8):
                sp.wait_ge(parts_out[at], 16 * SPL)

            def expert_out(g, f, last):
                sp.wait_ge(aux_free, aux_count(g, ("y", f), last))
                sp.dma_start(ye_d[bass.ds((g * EG + f) * CAP, CAP), :], ye[:, f, :]).then_inc(ye_out[f], 16)

            def body(g, pr, last):
                if not last:
                    sp.wait_ge(acc_full, g * NC)
                    load_stage(g + 1, 1 - pr)
                for f in range(EG):
                    expert_out(g, f, last)
                    if not last:
                        sp.wait_ge(aux_full, aux_count(g, ("y", f), False))
                        sp.dma_start(w13_sb[:, f, :, :], w13[bass.ds((g + 1) * EG + f, 1), :, :]
                                     .rearrange("o (k p) i -> p (o k) i", p=P)).then_inc(w_in[f], 16)
                        sp.dma_start(w2_sb[:, f, :, :], w2[bass.ds((g + 1) * EG + f, 1), :, :]
                                     .rearrange("o (k p) d -> p (o k) d", p=I2)).then_inc(w_in[f], 16)
                if not last:
                    for ic in range(NC):
                        shift_rows(g, ic, 1 - pr)

            with sp.Fori(0, NG // 2 - 1) as it:
                body(it * 2, 0, False)
                body(it * 2 + 1, 1, False)
            body(NG - 2, 0, False)
            body(NG - 1, 1, True)
            for n in range(NT):
                sp.wait_ge(y_done, n + 1)
                sp.dma_start(out[n * P:(n + 1) * P, :], acc[:, n, :]).then_inc(y_out, 16)
            sp.wait_ge(y_out, 16 * NT)

        @block.scalar
        def _(act):
            A = nc.scalar.activation
            for dst, src in ((pos[:, :], positions), (dire[:, :], directions), (LS, log_scales), (LA, log_amplitudes)):
                act.dma_start(dst, src).then_inc(par_in, 16)
            for dst, src in ((PS, sensitivity), (DS, strength), (GG, gsa_gate)):
                act.dma_start(dst, src.to_broadcast((P, 1))).then_inc(par_in, 16)
            act.dma_start(gw_sb[:, :, :], gate_w.rearrange("(k p) e -> p k e", p=P)).then_inc(gate_in, 16)
            act.dma_start(gb_sb[:, 0, :], gate_b.to_broadcast((P, E))).then_inc(gate_in, 16)
            act.wait_ge(consts, 1)
            act.dma_start(ids_d[0:DUMP, :].rearrange("(e c) o -> e (c o)", c=CAP), zero_i[:, :]).then_inc(ids0_out, 16)

            act.wait_ge(norm_ready, 1)
            A(NRM, NSQ, ACT.Sqrt).then_inc(norm_root, 1)
            act.wait_ge(var_ready, 1)
            A(vstd[:, 1, :], vstd[:, 0, :], ACT.Sqrt).then_inc(var_root, 1)

            def bank_ready(n):
                act.wait_ge(pro_full, n + 1)
                return ps[:, n % PB, :]

            def evacuate(n):
                kind, a = PRO[n]
                b = bank_ready(n)
                if kind == "xnT":
                    k, tq = a
                    A(xnT[:, k, tq * CH:(tq + 1) * CH], b, ACT.Copy).then_inc(pro_act, 1)
                elif kind == "proj":
                    s, m, tc = a
                    A(qkT[:, s, m, tc * CH:(tc + 1) * CH], b, ACT.Copy).then_inc(pro_act, 1)
                elif kind == "feat":
                    s, tc, w = a
                    A(feat[:, s, w, tc * CH:(tc + 1) * CH], b, ACT.Exp if w == 0 else ACT.Tanh,
                      bias=BG if w == 0 else BD).then_inc(pro_act, 1)
                else:
                    A(v_all[:, 2 * a:2 * a + 2, :].rearrange("p n d -> p (n d)"), b, ACT.Copy).then_inc(v_done, 1)

            def part0(at):
                n, m = SPLIT_ORDER[at]
                src = qkT[:, n, m, :] if n < 2 else feat[:, n - 2, m, :]
                if n < 2:
                    act.wait_ge(pro_act, reads[PRO.index(("proj", (n, m, 1)))][1])
                else:
                    act.wait_ge(features, n - 1)
                A(split[:, n, 0, m, :], src, ACT.Copy, scale=0.25 if n == 0 else 1.0).then_inc(first_part, 1)

            tasks = [n for n, (k, _) in enumerate(PRO) if READER[k] == "act"]
            for n in tasks[:4]:
                evacuate(n)
            act.wait_ge(par_in, 16 * 7)
            A(IS2, LS, ACT.Exp, scale=-2.0)
            A(AMP, LA, ACT.Exp)
            A(EG_, GG, ACT.Exp, scale=-1.0).then_inc(par_exp, 1)
            act.wait_ge(gate_dve, 1)
            A(g_[2][:, :, :], g_[1][:, :, :], ACT.Exp, scale=-1.0).then_inc(gate_act, 1)
            evacuate(tasks[4])
            act.wait_ge(gate_dve, 2)
            A(g_[4][:, :, :], g_[3][:, :, :], ACT.Ln).then_inc(gate_act, 1)
            evacuate(tasks[5])
            evacuate(tasks[6])
            act.wait_ge(gate_dve, 3)
            A(g_[10][:, :, :], g_[11][:, :, :], ACT.Sqrt).then_inc(gate_act, 1)
            evacuate(tasks[7])
            part0(0)
            part0(1)
            for n in tasks[8:12]:
                evacuate(n)
            act.wait_ge(gw_ready, 1)
            for n in tasks[12:20]:
                evacuate(n)
            for at in range(2, 2 * 4):
                if at == 4:
                    for n in tasks[20:]:
                        evacuate(n)
                part0(at)

            act.wait_ge(parts_ready, 2 * 4)

            def body(g, last):
                tanh_at = {}
                for p in range(NP + 1):
                    for t in (LAST if last else AUX)[p]:
                        if t[0] == "gu":
                            tanh_at.setdefault(p, []).append(t)
                for p, (ic, jb) in enumerate(PAIRS):
                    def exps(var):
                        ready, done = (std_ready, std_exp) if var == 0 else (gsa_ready, gsa_exp)
                        for s in range(2):
                            off, _ = shape_of(ic, jb + s)
                            act.wait_ge(ready, g * (2 * NP) + (2 * p + s + 1))
                            A(probs[:, var, s, :, off:CH], ps[:, 2 + 2 * s:4 + 2 * s, off:CH], ACT.Exp).then_inc(done, 1)
                    exps(0)
                    exps(1)
                    for t in tanh_at.get(p, []):
                        f = t[1]
                        act.wait_ge(aux_full, aux_count(g, t, last))
                        A(th[:, :], ps[:, aux_bank(g, t, last), 0:I], ACT.Tanh, scale=0.5).then_inc(th_ready, 1)

            with act.Fori(0, NG - 1) as g:
                body(g, False)
            body(NG - 1, True)

        @block.tensor
        def _(pe):
            M = nc.tensor.matmul
            pe.wait_ge(consts, 1)

            def take(n):
                if n >= PB:
                    s, c = reads[n - PB]
                    if PRO[n - PB][0] == "v":
                        s = v_done
                    pe.wait_ge(s, c)
                return ps[:, n % PB, :]

            for n, (kind, a) in enumerate(PRO):
                b = take(n)
                if kind == "xnT":
                    k, tq = a
                    for i in range(TC):
                        t = tq * TC + i
                        pe.wait_ge(xn_ready, t + 1)
                        last = nc.tensor.transpose(b[:, i * P:(i + 1) * P], xn[:, t, k * P:(k + 1) * P], ident[:, :])
                elif kind == "par":
                    pe.wait_ge(gw_ready, 1)
                    for w in range(3):
                        last = nc.tensor.transpose(b[:, w * P:(w + 1) * P], gwide[:, w, :], ident[:, :])
                elif kind == "gate":
                    pe.wait_ge(gate_in, 32)
                    pe.wait_ge(pro_act, KD * NC)
                    for t in range(NT):
                        for k in range(KD):
                            last = M(b[:, t * E:(t + 1) * E], xnT[:, k, t * P:(t + 1) * P], gw_sb[:, k, :],
                                     start=k == 0, stop=k == KD - 1)
                elif kind == "proj":
                    s, m, tc = a
                    pe.wait_ge(wqk_in, 32)
                    for k in range(KD):
                        last = M(b, wt[:, s, k, m * P:(m + 1) * P], xnT[:, k, tc * CH:(tc + 1) * CH],
                                 start=k == 0, stop=k == KD - 1)
                elif kind == "feat":
                    s, tc, w = a
                    pe.wait_ge(pro_dve, 1)
                    pe.wait_ge(squares, 2 * s + 2)
                    for m in range(KD):
                        half = slice(64 * m, 64 * m + 64)
                        cols = slice(tc * CH, (tc + 1) * CH)
                        if w == 0:
                            M(b[half, :], gT[:, 0, half], sq[:, s, m, cols], start=True, stop=False)
                            last = M(b[half, :], gT[:, 1, half], qkT[:, s, m, cols], start=False, stop=True)
                        else:
                            last = M(b[half, :], gT[:, 2, half], qkT[:, s, m, cols], start=True, stop=True)
                elif kind == "cum":
                    pe.wait_ge(ohs_ready, 1)
                    M(b[:, 0:NT * E], upper[:, :], ohs[:, :, :].rearrange("p n e -> p (n e)"), start=True, stop=False)
                    for t in range(NT - 1):
                        rest = NT - 1 - t
                        last = M(b[:, (t + 1) * E:NT * E].rearrange("p (n e) -> p n e", e=E), ones_b[:, :],
                                 ohs[:, t:t + 1, :].to_broadcast((P, rest, E)), start=False, stop=t == NT - 2)
                else:
                    pe.wait_ge(wvo_in, 32)
                    for i in range(2):
                        for k in range(KD):
                            last = M(b[:, i * D:(i + 1) * D], xnT[:, k, (2 * a + i) * P:(2 * a + i + 1) * P],
                                     wt[:, 2, k, :], start=k == 0, stop=k == KD - 1)
                last.then_inc(pro_full, 1)

            def aux(g, t, last, pr):
                kind, a = t
                bank = aux_bank(g, t, last)
                b = ps[:, bank, :]
                count = aux_count(g, t, last)
                if not isinstance(count, int) or count > 2:
                    pe.wait_ge(aux_free, count - 2)
                if kind == "max":
                    h, it, pc = a
                    n0, n1 = pc * CH, min((it + 1) * P, (pc + 1) * CH)
                    diag = n1 == (it + 1) * P
                    lhs = qs[0:KR, pr, h, it * P:(it + 1) * P]
                    ins = M(b[:, 0:n1 - n0], lhs, ks[0:KR, pr, h, n0:n1], start=True, stop=not diag)
                    if diag:
                        ins = M(b[:, n1 - n0 - P:n1 - n0], ident_b[:, :], mask_n[:, :], start=False, stop=True)
                elif kind == "shift":
                    pe.wait_ge(mhl_ready, (g + 1) * NC + (a + 1))
                    ins = nc.tensor.transpose(psb[0:2 * GH * TC, bank, 0:P],
                                              mhl[:, a, :, :].rearrange("p s c -> p (s c)"), ident_b[:, :])
                elif kind == "xT":
                    if a < EG:
                        pe.wait_ge(xe_in[a], (g + 1) * 16)
                        for k in range(KD):
                            ins = nc.tensor.transpose(b[:, k * P:(k + 1) * P], xe[:, a, k * P:(k + 1) * P], ident[:, :])
                    else:
                        pe.wait_ge(xs_ready, g + 1)
                        for k in range(KD):
                            ins = nc.tensor.transpose(b[:, k * P:(k + 1) * P], xs[:, k * P:(k + 1) * P], ident[:, :])
                elif kind == "gu":
                    pe.wait_ge(aux_free, aux_count(g, ("xT", a), last))
                    if a < EG:
                        pe.wait_ge(w_in[a], (g + 1) * 32)
                    else:
                        pe.wait_ge(ws_in, 32)
                    for k in range(KD):
                        ins = M(b[:, 0:2 * I], xeT[:, k, :], w13_sb[:, a, k, :], start=k == 0, stop=k == KD - 1)
                elif kind == "hT":
                    pe.wait_ge(aux_free, aux_count(g, ("gu", a), last))
                    for c in range(2):
                        ins = nc.tensor.transpose(b[0:I2, c * P:(c + 1) * P], hh[:, c * I2:(c + 1) * I2], ident[:, :])
                elif kind == "y":
                    pe.wait_ge(aux_free, aux_count(g, ("hT", a), last))
                    for c in range(2):
                        ins = M(b[:, 0:D], hT[:, c, :], w2_sb[:, a, c, :], start=c == 0, stop=c == 1)
                else:
                    pe.wait_ge(acc_free, g * NC + (a + 3))
                    for i in range(TC):
                        ins = nc.tensor.transpose(b[:, i * P:(i + 1) * P], pv_sb[:, i * P:(i + 1) * P], ident[:, :])
                ins.then_inc(aux_full, 1)

            pe.wait_ge(qk_in[0], 96)
            for t in PRE:
                aux(-1, t, False, 0)

            def body(g, pr, last, half):
                plan = LAST if last else AUX
                nhalf = half + pr

                def std(p, s):
                    ic, jb = PAIRS[p]
                    off, diag = shape_of(ic, jb + s)
                    if s == 0 and jb == 0:
                        pe.wait_ge(shift_in[ic], (g + 1) * 64)
                    if p:
                        pe.wait_ge(gsa_exp, g * (2 * NP) + (2 * (p - 1) + s + 1))
                    else:
                        pe.wait_ge(gsa_exp, g * (2 * NP))
                    for h in range(GH):
                        b = ps[:, 2 + 2 * s + h, :]
                        ins = M(b[:, off:CH], ks[:, pr, h, (jb + s) * P:(jb + s + 1) * P],
                                qs[:, pr, h, ic * CH + off:(ic + 1) * CH], start=True, stop=not diag)
                        if diag:
                            ins = M(b[:, off:off + P], ident_b[:, :], mask_t[:, :], start=False, stop=True)
                    ins.then_inc(std_ready, 1)

                def splat(p, s):
                    ic, jb = PAIRS[p]
                    off, _ = shape_of(ic, jb + s)
                    pe.wait_ge(std_exp, g * (2 * NP) + (2 * p + s + 1))
                    for h in range(GH):
                        ins = M(ps[:, 2 + 2 * s + h, off:CH], fk[:, pr, h, (jb + s) * P:(jb + s + 1) * P],
                                fq[:, pr, h, ic * CH + off:(ic + 1) * CH], start=False, stop=True,
                                skip_group_check=True)
                    ins.then_inc(gsa_ready, 1)

                def pv(p, s):
                    ic, jb = PAIRS[p]
                    off, _ = shape_of(ic, jb + s)
                    if jb + s == 0:
                        pe.wait_ge(acc_free, g * NC + (ic + 1))
                        pe.wait_ge(v_ready, g + 1)
                    pe.wait_ge(gsa_exp, g * (2 * NP) + (2 * p + s + 1))
                    end = jb + s == (ic + 1) * TC - 1
                    for var in range(2):
                        for h in range(GH):
                            c = 2 * HD * (var * GH + h)
                            ins = M(ps[c:c + 2 * HD, ic, off:CH], v_st[:, pr, jb + s, h, :],
                                    probs[:, var, s, h, off:CH], start=jb + s == 0, stop=end)
                    if end:
                        ins.then_inc(acc_full, 1)

                def some(p, share, of):
                    a = plan[p]
                    for t in a[len(a) * share // of:len(a) * (share + 1) // of]:
                        if t[0] == "max":
                            pe.wait_ge(qk_in[1 - pr], (nhalf + 1) * 96)
                        aux(g, t, last, 1 - pr)

                pe.wait_ge(f_in[pr], (half + 1) * 96)
                std(0, 0)
                std(0, 1)
                for p in range(NP):
                    some(p, 0, 4)
                    splat(p, 0)
                    some(p, 1, 4)
                    splat(p, 1)
                    some(p, 2, 4)
                    pv(p, 0)
                    if p + 1 < NP:
                        std(p + 1, 0)
                    some(p, 3, 4)
                    pv(p, 1)
                    if p + 1 < NP:
                        std(p + 1, 1)
                some(NP, 0, 1)

            with pe.Fori(0, NG // 2 - 1) as it:
                body(it * 2, 0, False, it)
                body(it * 2 + 1, 1, False, it)
            body(NG - 2, 0, False, NG // 2 - 1)
            body(NG - 1, 1, True, NG // 2 - 1)

            pe.wait_ge(o_ready, NG * NC)
            pe.wait_ge(wvo_in, 32)
            for n in range(2 * NC):
                k, tq = n // NC, n % NC
                b = ps[:, n, :]
                for i in range(TC):
                    ins = nc.tensor.transpose(b[:, i * P:(i + 1) * P], o_nat[:, tq * TC + i, k * P:(k + 1) * P], ident[:, :])
                ins.then_inc(oT_full, 1)
            for n in range(NT):
                pe.wait_ge(oT_ready, 4 if n >= TC else 4)
                b = ps[:, 4 + n % 4, 0:D]
                if n >= 4:
                    pe.wait_ge(y_done, n - 3)
                for k in range(KD):
                    ins = M(b, oT[:, k, n * P:(n + 1) * P], wt[:, 3, k, :], start=k == 0, stop=k == KD - 1)
                ins.then_inc(y_full, 1)

        @block.vector
        def _(dve):
            V = nc.vector
            steps, base = [0], [0]

            def link(ins):
                steps[0] += 1
                ins.then_inc(dve_step, 1)
                dve.wait_ge(dve_step, base[0] + steps[0])

            def tt(out, a, b, op):
                return V.tensor_tensor(out, a, b, op)

            dve.wait_ge(par_in, 16 * 7)
            tt(tmp16[:, 0, :], dire[:, :], dire[:, :], ALU.mult)
            link(tt(tmp16[:, 1, :], pos[:, :], pos[:, :], ALU.mult))
            V.reduce_sum(PP, tmp16[:, 1, :], AX.X)
            V.reduce_sum(NSQ, tmp16[:, 0, :], AX.X).then_inc(norm_ready, 1)
            for t in range(NT):
                dve.wait_ge(x_in[t // TC], 16)
                ins = V.bn_stats(stats[:, t, :], acc[:, t, :])
            link(ins)
            for t in range(NT):
                ins = V.bn_aggr(mv[:, t, :], stats[:, t, :])
            link(ins)
            V.tensor_scalar(vstd[:, 0, :], mv[:, :, 1], EPS, None, ALU.add).then_inc(var_ready, 1)
            dve.wait_ge(var_root, 1)
            link(V.reciprocal(vstd[:, 0, :], vstd[:, 1, :]))
            for t in range(NT):
                V.tensor_scalar(xn[:, t, :], acc[:, t, :], mv[:, t, 0:1], vstd[:, 0, t:t + 1],
                                ALU.subtract, ALU.mult).then_inc(xn_ready, 1)
            dve.wait_ge(norm_root, 1)
            dve.wait_ge(par_exp, 1)
            dve.wait_ge(consts, 1)
            link(V.tensor_scalar(TMP, NRM, 1e-8, None, ALU.add))
            link(V.reciprocal(RN, TMP))
            V.tensor_scalar(HI2, IS2, -0.5, None, ALU.mult)
            V.tensor_scalar(tmp16[:, 3, :], pos[:, :], IS2, None, ALU.mult)
            V.tensor_scalar(C1, AMP, PS, None, ALU.mult)
            V.tensor_scalar(B1_, EG_, 1.0, None, ALU.add)
            link(V.tensor_scalar(tmp16[:, 2, :], dire[:, :], RN, None, ALU.mult))
            V.tensor_scalar(C2, C1, DS, None, ALU.mult)
            V.tensor_scalar(BG, HI2, PP, None, ALU.mult)
            V.reciprocal(B_, B1_)
            V.tensor_scalar(gwide[:, 0, :], blockm[:, :, :].rearrange("p h d -> p (h d)"), HI2, None, ALU.mult)
            tt(gwide[:, 1, :].rearrange("p (h d) -> p h d", d=HD), blockm[:, :, :],
               tmp16[:, 3:4, :].to_broadcast((P, NS, HD)), ALU.mult)
            tt(gwide[:, 2, :].rearrange("p (h d) -> p h d", d=HD), blockm[:, :, :],
               tmp16[:, 2:3, :].to_broadcast((P, NS, HD)), ALU.mult)
            link(tt(tmp16[:, 0, :], pos[:, :], tmp16[:, 2, :], ALU.mult))
            V.tensor_scalar(blendw[:, 2:3], B_, 0.15, 0.03, ALU.mult, ALU.min)
            link(V.reduce_sum(PD, tmp16[:, 0, :], AX.X))
            V.tensor_scalar(blendw[:, 3:4], blendw[:, 2:3], 1.0, None, ALU.mult)
            V.tensor_scalar(blendw[:, 0:1], blendw[:, 2:3], -1.0, 1.0, ALU.mult, ALU.add)
            V.tensor_scalar(blendw[:, 1:2], blendw[:, 2:3], -1.0, 1.0, ALU.mult, ALU.add)
            V.tensor_scalar(BD, PD, -1.0, None, ALU.mult).then_inc(gw_ready, 1)
            n = PRO.index(("par", 0))
            dve.wait_ge(pro_full, n + 1)
            V.tensor_copy(gT[:, :, :].rearrange("p w c -> p (w c)"), ps[:, n % PB, 0:3 * P]).then_inc(pro_dve, 1)
            n = PRO.index(("gate", 0))
            dve.wait_ge(pro_full, n + 1)
            flat = ps[:, n % PB, 0:NT * E].rearrange("p (n e) -> p n e", e=E)
            G = [g[:, :, :] for g in g_]
            R = [r_[:, n, :] for n in range(16)]

            def row(r):
                return r.unsqueeze(2).to_broadcast((P, NT, E))
            V.tensor_copy(G[0], flat).then_inc(pro_dve, 1)
            dve.wait_ge(pro_dve, 2)
            V.scalar_tensor_tensor(out=G[1], in0=G[0], scalar=-1.0, in1=G[0], op0=ALU.mult, op1=ALU.max).then_inc(gate_dve, 1)
            V.tensor_scalar(G[5], G[0], 0.0, None, ALU.max)
            dve.wait_ge(gate_act, 1)
            V.tensor_scalar(G[3], G[2], 1.0, None, ALU.add).then_inc(gate_dve, 1)
            dve.wait_ge(gate_dve, 2)
            link(V.tensor_scalar(G[6], G[3], -1.0, None, ALU.add))
            link(V.tensor_scalar(G[7], G[6], 0.0, None, ALU.is_equal))
            link(tt(G[6], G[6], G[7], ALU.add))
            V.reciprocal(G[8], G[6])
            link(tt(G[9], G[7], G[2], ALU.mult))
            link(tt(G[8], G[8], G[2], ALU.mult))
            dve.wait_ge(gate_act, 2)
            link(tt(G[8], G[8], G[4], ALU.mult))
            link(tt(G[8], G[8], G[9], ALU.add))
            tt(G[11], G[8], G[5], ALU.add).then_inc(gate_dve, 1)
            dve.wait_ge(gate_act, 3)
            link(tt(G[11], G[10], gb_sb[:, :, :].to_broadcast((P, NT, E)), ALU.add))
            choose, score, oh = G[11], G[10], [G[2], G[5]]
            for k in range(2):
                link(V.reduce_max(R[0], choose, AX.X))
                link(tt(G[1], choose, row(R[0]), ALU.is_ge))
                link(tt(G[1], G[1], iota_r[:, :, :], ALU.mult))
                link(V.reduce_max(R[1], G[1], AX.X))
                link(tt(oh[k], G[1], row(R[1]), ALU.is_equal))
                if k == 0:
                    link(V.scalar_tensor_tensor(out=choose, in0=oh[0], scalar=NEG, in1=choose, op0=ALU.mult, op1=ALU.add))
                link(tt(G[1], oh[k], score, ALU.mult))
                link(V.reduce_sum(R[2 + k], G[1], AX.X))
            tt(ohs[:, :, :], oh[0], oh[1], ALU.add).then_inc(ohs_ready, 1)
            link(tt(R[4], R[2], R[3], ALU.add))
            link(V.reciprocal(R[5], R[4]))

            def slots():
                n = PRO.index(("cum", 0))
                dve.wait_ge(pro_full, n + 1)
                V.tensor_copy(G[7], ps[:, n % PB, 0:NT * E].rearrange("p (n e) -> p n e", e=E)).then_inc(pro_dve, 1)
                dve.wait_ge(pro_dve, 3)
                link(tt(G[8], G[7], iota_s[:, :, :], ALU.add))
                for k in range(2):
                    tt(G[9], oh[k], G[7], ALU.mult)
                    link(tt(G[1], oh[k], G[8], ALU.mult))
                    V.reduce_sum(R[6], G[9], AX.X)
                    link(V.reduce_sum(R[7], G[1], AX.X))
                    link(V.tensor_scalar(R[8], R[6], float(CAP), None, ALU.is_lt))
                    tt(R[9], R[2 + k], R[5], ALU.mult)
                    tt(R[10], R[7], R[8], ALU.mult)
                    link(tt(R[11], R[7], dump[:, k, :], ALU.subtract))
                    tt(pairw[:, k, :], R[9], R[8], ALU.mult)
                    V.tensor_copy(gidx[:, k, :], R[10])
                    link(tt(R[12], R[11], R[8], ALU.mult))
                    link(tt(R[13], R[12], dump[:, k, :], ALU.add))
                    V.tensor_copy(sidx[:, k, :], R[13]).then_inc(slots_ready, 1)

            def parts(at):
                n, m = SPLIT_ORDER[at]
                src = qkT[:, n, m, :] if n < 2 else feat[:, n - 2, m, :]
                dve.wait_ge(first_part, at + 1)
                link(V.scalar_tensor_tensor(out=rest_[:, 0, :], in0=src, scalar=0.25 if n == 0 else 1.0, in1=split[:, n, 0, m, :],
                                            op0=ALU.mult, op1=ALU.subtract))
                link(V.tensor_copy(split[:, n, 1, m, :], rest_[:, 0, :]))
                link(tt(rest_[:, 1, :], rest_[:, 0, :], split[:, n, 1, m, :], ALU.subtract))
                V.tensor_copy(split[:, n, 2, m, :], rest_[:, 1, :]).then_inc(parts_ready, 1)

            parts(0)
            parts(1)
            for s in range(2):
                for m in range(KD):
                    dve.wait_ge(pro_act, reads[PRO.index(("proj", (s, m, 1)))][1])
                    tt(sq[:, s, m, :], qkT[:, s, m, :], qkT[:, s, m, :], ALU.mult).then_inc(squares, 1)
            for s in range(2):
                dve.wait_ge(pro_act, reads[PRO.index(("feat", (s, 1, 1)))][1])
                gs, dr = feat[:, s, 0, :], feat[:, s, 1, :]
                if s == 0:
                    link(V.scalar_tensor_tensor(out=dr, in0=gs, scalar=C2, in1=dr, op0=ALU.mult, op1=ALU.mult))
                    V.tensor_scalar(gs, gs, C1, None, ALU.mult).then_inc(features, 1)
                else:
                    tt(dr, gs, dr, ALU.mult).then_inc(features, 1)
            slots()
            for at in range(2, 8):
                parts(at)
            V.memset(mx[:, :, :, :, :], 0.0).then_inc(acc_free, 2)
            dve.wait_ge(acc_free, 2)

            def aux(g, t, last):
                kind, a = t
                bank = aux_bank(g, t, last)
                b = ps[:, bank, :]
                dve.wait_ge(aux_full, aux_count(g, t, last))
                if kind == "max":
                    h, it, pc = a
                    n0, n1 = pc * CH, min((it + 1) * P, (pc + 1) * CH)
                    V.reduce_max(mx[:, it // TC, h, it % TC, pc:pc + 1], b[:, 0:n1 - n0], AX.X).then_inc(aux_free, 1)
                    if t == max0[-1] or t == max1[-1]:
                        ic = it // TC
                        dve.wait_ge(aux_free, aux_count(g, t, last))
                        if ic == 0:
                            link(V.tensor_scalar(mneg[:, 0, :, :], mx[:, 0, :, :, 0], -1.0, None, ALU.mult))
                        else:
                            link(tt(mneg[:, 0, :, :], mx[:, 1, :, :, 0], mx[:, 1, :, :, 1], ALU.max))
                            link(V.tensor_scalar(mneg[:, 0, :, :], mneg[:, 0, :, :], -1.0, None, ALU.mult))
                        m32 = mneg[:, 0, :, :].rearrange("p h n -> p (h n)")
                        link(V.tensor_copy(mhl[:, ic, 0, :], m32))
                        tt(mhl[:, ic, 1, :], m32, mhl[:, ic, 0, :], ALU.subtract).then_inc(mhl_ready, 1)
                elif kind == "shift":
                    if not isinstance(g, int) or g >= 0:
                        dve.wait_ge(shift_in[a], (g + 1) * 64)
                    V.tensor_copy(mT[:, a, :], psb[0:2 * GH * TC, bank, 0:P]).then_inc(aux_free, 1)
                elif kind == "xT":
                    V.tensor_copy(xeT[:, :, :].rearrange("p k c -> p (k c)"), b[:, 0:D]).then_inc(aux_free, 1)
                elif kind == "gu":
                    dve.wait_ge(th_ready, g * NF + (a + 1))
                    link(V.scalar_tensor_tensor(out=h1[:, :], in0=th[:, :], scalar=1.0, in1=b[:, 0:I], op0=ALU.add, op1=ALU.mult))
                    V.scalar_tensor_tensor(out=hh[:, :], in0=h1[:, :], scalar=0.5, in1=b[:, I:2 * I], op0=ALU.mult, op1=ALU.mult).then_inc(aux_free, 1)
                elif kind == "hT":
                    V.tensor_copy(hT[:, :, :].rearrange("p k c -> p (k c)"), b[0:I2, 0:2 * P]).then_inc(aux_free, 1)
                elif kind == "y":
                    if a < EG:
                        dve.wait_ge(ye_out[a], g * 16)
                        V.tensor_copy(ye[:, a, :], b[:, 0:D]).then_inc(aux_free, 1)
                    else:
                        dst = acc[:, bass.ds(g, 1), :].rearrange("p o d -> p (o d)")
                        tt(dst, b[:, 0:D], dst, ALU.add).then_inc(aux_free, 1)
                else:
                    o4 = b[:, :].rearrange("p (n v c) -> p n v c", n=TC, v=4)
                    link(V.reciprocal(rec[:, :, :], o4[:, :, :, HD]))
                    link(tt(recw[:, :, :], rec[:, :, :], blendw[:, :].unsqueeze(1).to_broadcast((P, TC, 4)), ALU.mult))
                    tt(onv[:, :, :, :], o4[:, :, :, 0:HD], recw[:, :, :].unsqueeze(3).to_broadcast((P, TC, 4, HD)), ALU.mult).then_inc(aux_free, 1)
                    dve.wait_ge(aux_free, aux_count(g, t, last))
                    dst = o_nat[:, a * TC:(a + 1) * TC, bass.ds(g * (GH * HD), GH * HD)].rearrange("p n (h d) -> p n h d", h=GH)
                    tt(dst, onv[:, :, 0:2, :], onv[:, :, 2:4, :], ALU.add).then_inc(o_ready, 1)

            for t in PRE:
                aux(-1, t, False)

            def body(g, last):
                base[0] = LINKS0 + LINKS * g if not last else LINKS0 + LINKS * (NG - 1)
                start = steps[0] = 0
                plan = LAST if last else AUX
                V.tensor_copy(xs[:, :], xn[:, bass.ds(g, 1), :].rearrange("p o d -> p (o d)")).then_inc(xs_ready, 1)
                for p in range(NP + 1):
                    for t in plan[p]:
                        if t[0] == "oT":
                            dve.wait_ge(acc_full, g * NC + (t[1] + 1))
                            V.tensor_copy(pv_sb[:, :], ps[:, t[1], :]).then_inc(acc_free, 1)
                        aux(g, t, last)
                return steps[0]

            LINKS0 = steps[0]
            LINKS = sum({"gu": 1, "oT": 2}.get(t[0], 0) + (2 if t == max0[-1] else 3 if t == max1[-1] else 0) for t in FLAT)
            with dve.Fori(0, NG - 1) as g:
                used = body(g, False)
            assert used == LINKS, (used, LINKS)
            body(NG - 1, True)

            for n in range(2 * NC):
                k, tq = n // NC, n % NC
                dve.wait_ge(oT_full, n + 1)
                V.tensor_copy(oT[:, k, tq * CH:(tq + 1) * CH], ps[:, n, :]).then_inc(oT_ready, 1)
            for n in range(NT):
                dve.wait_ge(gath_in[n % 2], 32 * (n // 2 + 1))
                for k in range(2):
                    ins = V.scalar_tensor_tensor(out=acc[:, n, :], in0=gath[:, k, n % 2, :], scalar=pairw[:, k, n:n + 1],
                                                 in1=acc[:, n, :], op0=ALU.mult, op1=ALU.add)
                    ins.then_inc(gath_used, 1)
                    dve.wait_ge(gath_used, 2 * n + k + 1)
                dve.wait_ge(y_full, n + 1)
                tt(acc[:, n, :], ps[:, 4 + n % 4, 0:D], acc[:, n, :], ALU.add).then_inc(y_done, 1)

    return nc


_INS = ["x", "wqkvo", "positions", "directions", "log_scales", "log_amplitudes", "strength", "sensitivity",
        "gsa_gate", "gate_w", "gate_b", "w13", "w2", "ws13", "ws2"]


def kernel(**inputs):
    import numpy as np
    import concourse.bacc as bacc
    from concourse import mybir as mb
    from concourse.bass_utils import run_bass_kernel_spmd as run

    def a(name):
        return np.asarray(inputs[name])

    def c(v):
        return np.ascontiguousarray(v)

    x = a("L0_attn_hidden_states")
    w = [a("L0_attn_" + n) for n in ("Wq", "Wk", "Wv", "Wo")]
    W1, W3, W2 = a("L0_ffn_W1"), a("L0_ffn_W3"), a("L0_ffn_W2")
    laid = {
        "x": x.reshape(x.shape[1], x.shape[2]),
        "wqkvo": np.stack([m.T for m in w]),
        "positions": a("L0_attn_splat_positions").reshape(128, 16),
        "directions": a("L0_attn_splat_directions").reshape(128, 16),
        "log_scales": a("L0_attn_splat_log_scales").reshape(128, 1),
        "log_amplitudes": a("L0_attn_splat_log_amplitudes").reshape(128, 1),
        "strength": a("L0_attn_directional_strength").reshape(1, 1),
        "sensitivity": a("L0_attn_position_sensitivity").reshape(1, 1),
        "gsa_gate": a("L0_attn_gsa_strength").reshape(1, 1),
        "gate_w": a("L0_ffn_gate_w").T,
        "gate_b": a("L0_ffn_gate_b").reshape(1, -1),
        "w13": np.concatenate([W1.transpose(0, 2, 1), W3.transpose(0, 2, 1)], axis=2),
        "w2": W2.transpose(0, 2, 1),
        "ws13": np.concatenate([a("L0_ffn_Ws1").T, a("L0_ffn_Ws3").T], axis=1),
        "ws2": a("L0_ffn_Ws2").T,
    }
    nc = bacc.Bacc("TRN2", target_bir_lowering=False, num_devices=1)
    arrays, args = {}, []
    for name in _INS:
        v = c(laid[name])
        arrays[f"in_{name}_dram"] = v
        args.append(nc.dram_tensor(f"in_{name}_dram", v.shape, mb.dt.from_np(v.dtype), kind="ExternalInput").ap())
    out = nc.dram_tensor("out_dram", (x.shape[1], x.shape[2]), mb.dt.from_np(x.dtype), kind="ExternalOutput").ap()
    bass_splat_attention_moe_layer(nc, *args, out)
    r = run(nc, [arrays], core_ids=[0])
    return r.results[0]["out_dram"].reshape(x.shape)
```

```python
from contextlib import ExitStack

import concourse.bass as bass
from concourse import mybir


def bass_splat_attention_moe_layer(nc, x, wqkvo, positions, directions, log_scales, log_amplitudes,
                                   strength, sensitivity, gsa_gate, gate_w, gate_b,
                                   w13, w2, ws13, ws2, out):
    f32, bf16, u32 = mybir.dt.float32, mybir.dt.bfloat16, mybir.dt.uint32
    ALU, ACT, AX = mybir.AluOpType, mybir.ActivationFunctionType, mybir.AxisListType

    T, D = x.shape
    P = 128
    NT = T // P
    KD = D // P
    H, NS, HD = 16, 8, 16
    E, I, CAP = 16, 176, 128
    I2 = I // 2
    CH = 512
    NC = T // CH
    TC = CH // P
    GH = 2
    NG = H // GH
    NH = NG // 2
    EG = E // NH
    SG = NT // NH
    SPL = 3
    RUNS = [(0, 0, 3, 0), (3, 0, 2, 1), (5, 0, 1, 2)]
    KR = HD * 6
    KS = KR + 2
    NEG = -1.0e30
    DUMP = E * CAP
    EPS = 1e-5

    xn_d = nc.dram_tensor("xn_scratch", (T, D), f32).ap()
    ids_d = nc.dram_tensor("ids_scratch", (DUMP + 2 * T, 1), u32).ap()
    ye_d = nc.dram_tensor("ye_scratch", (E * CAP, D), f32).ap()
    parts_d = [nc.dram_tensor(f"parts_scratch{n}", (H, SPL, HD, T), bf16).ap() for n in range(4)]

    ctx = ExitStack()
    with ctx:
        def sb(name, shape, dt):
            return ctx.enter_context(nc.sbuf_tensor(name, shape, dt))

        def sem(name):
            return ctx.enter_context(nc.semaphore(name))

        acc = sb("acc", [P, NT, D], f32)
        xn = sb("xn", [P, NT, D], f32)
        xnT = sb("xnT", [P, KD, T], f32)
        wt = sb("wt", [P, 4, KD, D], f32)
        v_all = sb("v_all", [P, NT, D], f32)
        v_st = sb("v_st", [P, 2, NT, GH, 2 * HD], f32)
        stage = [sb(f"stage{n}", [KS, 2, GH, T], bf16) for n in range(4)]
        qs, ks, fq, fk = stage
        arena_p = sb("arena_p", [P, 4, 1024], f32)
        arena_o = sb("arena_o", [P, 4, T], f32)
        rest_ = sb("rest", [P, 2, T], f32)
        split = sb("split", [P, 4, SPL, 2, T], bf16)
        sq = split[:, 2:4, :, :, :].rearrange("p a b c t -> p (a b c t)").bitcast(f32)[:, 0:2 * KD * T] \
            .rearrange("p (s m t) -> p s m t", s=2, m=KD)
        qkT = arena_p[:, :, :].rearrange("p (s m) t -> p s m t", s=2)
        feat = arena_o[:, :, :].rearrange("p (s m) t -> p s m t", s=2)
        probs = arena_p[:, :, :].rearrange("p (v s) (h n) -> p v s h n", v=2, h=GH)
        GW = GH * HD
        o_nat = arena_o[:, :, :].rearrange("p a t -> p (a t)")[:, 0:NT * (D + GW)].rearrange("p (n d) -> p n d", d=D + GW)
        oT = rest_
        gath = split[:, :, :, :, :].rearrange("p a b c t -> p (a b c t)").bitcast(f32)[:, 0:2 * NT * D] \
            .rearrange("p (k n d) -> p k n d", k=2, n=NT)

        w13_sb = sb("w13_sb", [P, EG, KD, 2 * I], f32)
        w2_sb = sb("w2_sb", [I2, EG, 2, D], f32)
        xe = sb("xe", [P, EG, D], f32)
        xeT = sb("xeT", [P, KD, P], f32)
        th = sb("th", [P, I], f32)
        h1 = sb("h1", [P, I], f32)
        hh = sb("hh", [P, I], f32)
        hT = sb("hT", [I2, 2, P], f32)
        ye = sb("ye", [P, EG, D], f32)
        pv_sb = sb("pv_sb", [P, CH], f32)
        rec = sb("rec", [P, TC, 4], f32)
        recw = sb("recw", [P, TC, 4], f32)
        onv = sb("onv", [P, TC, 4, HD], f32)
        mx = sb("mx", [P, 2, GH, TC, 2], f32)
        mneg = sb("mneg", [P, 2, GH, TC], f32)
        mhl = sb("mhl", [P, 2, 2, GH * TC], bf16)
        mT = sb("mT", [2 * GH * TC, 2, P], bf16)

        ident = sb("ident", [P, P], f32)
        ident_b = sb("ident_b", [P, P], bf16)
        mask_t = sb("mask_t", [P, P], bf16)
        mask_n = sb("mask_n", [P, P], bf16)
        upper = sb("upper", [P, P], bf16)
        ones_b = sb("ones_b", [P, P], bf16)
        blockm = sb("blockm", [P, NS, HD], f32)
        iota_r = sb("iota_r", [P, NT, E], f32)
        iota_s = sb("iota_s", [P, NT, E], f32)
        iota_i = sb("iota_i", [P, 2, NT], u32)
        tok = sb("tok", [P, NT], u32)
        dump = sb("dump", [P, 2, NT], f32)
        zero_i = sb("zero_i", [E, CAP], u32)

        pos = sb("pos", [P, HD], f32)
        dire = sb("dire", [P, HD], f32)
        par = sb("par", [P, 24], f32)
        (LS, LA, PS, DS, GG, IS2, AMP, NSQ, NRM, RN, PD, PP, BG, C1, C2, BD, HI2, EG_, B_, B1_, TMP, TMP2) = \
            [par[:, n:n + 1] for n in range(22)]
        tmp16 = sb("tmp16", [P, 4, HD], f32)
        gwide = pv_sb[:, 0:3 * P].rearrange("p (w c) -> p w c", w=3)
        gT = sb("gT", [P, 3, P], f32)
        blendw = sb("blendw", [P, 4], f32)
        stats = sb("stats", [P, NT, 6], f32)
        mv = sb("mv", [P, NT, 2], f32)
        vstd = sb("vstd", [P, 2, NT], f32)
        gw_sb = sb("gw_sb", [P, KD, E], f32)
        gb_sb = sb("gb_sb", [P, 1, E], f32)
        g_ = [v_all[:, n // 2, (n % 2) * P:(n % 2 + 1) * P].rearrange("p (n e) -> p n e", e=E) for n in range(12)]
        ohs = sb("ohs", [P, NT, E], bf16)
        r_ = sb("r_", [P, 16, NT], f32)
        sidx = sb("sidx", [P, 2, NT], u32)
        gidx = sb("gidx", [P, 2, NT], u32)
        pairw = sb("pairw", [P, 2, NT], f32)
        ids_sb = sb("ids_sb", [P, E], u32)
        ids_cur = sb("ids_cur", [P, EG, 1], u32)

        ps = ctx.enter_context(nc.psum_tensor("ps", [P, 8, CH], f32))
        psb = ps[:, :, :].rearrange("p b n -> p (b n)").bitcast(bf16).rearrange("p (b n) -> p b n", b=8)

        par_in, wqk_in, wvo_in, gate_in, ws_in = (sem(n) for n in ("par_in", "wqk_in", "wvo_in", "gate_in", "ws_in"))
        consts = sem("consts")
        dve_step, pool_step = sem("dve_step"), sem("pool_step")
        x_in = [sem(f"x_in{n}") for n in range(NC)]
        pool_ids = sem("pool_ids")
        norm_ready, norm_root, var_ready, var_root = sem("norm_ready"), sem("norm_root"), sem("var_ready"), sem("var_root")
        xn_ready, par_exp, gw_ready, gate_dve, gate_act = (sem(n) for n in ("xn_ready", "par_exp", "gw_ready", "gate_dve", "gate_act"))
        ohs_ready, slots_ready, v_done = sem("ohs_ready"), sem("slots_ready"), sem("v_done")
        first_part, squares, features, parts_ready = sem("first_part"), sem("squares"), sem("features"), sem("parts_ready")
        pro_full = sem("pro_full")
        xn_out, ids0_out, ids_out, ids_in = sem("xn_out"), sem("ids0_out"), sem("ids_out"), sem("ids_in")
        parts_out = [sem(f"parts_out{n}") for n in range(8)]
        qk_in = [sem(f"qk_in{n}") for n in range(2)]
        f_in = [sem(f"f_in{n}") for n in range(2)]
        aux_full, aux_free = sem("aux_full"), sem("aux_free")
        std_ready, std_exp, gsa_ready, gsa_exp = sem("std_ready"), sem("std_exp"), sem("gsa_ready"), sem("gsa_exp")
        acc_full, acc_free, acc_one = sem("acc_full"), sem("acc_free"), sem("acc_one")
        o_ready = sem("o_ready")
        shift_in = [sem(f"shift_in{n}") for n in range(NC)]
        v_ready, mhl_ready = sem("v_ready"), sem("mhl_ready")
        xe_in = [sem(f"xe_in{n}") for n in range(EG)]
        w_in = [sem(f"w_in{n}") for n in range(EG)]
        th_ready = sem("th_ready")
        ye_out = [sem(f"ye_out{n}") for n in range(EG)]
        gath_in = [sem(f"gath_in{n}") for n in range(NT)]
        y_out = sem("y_out")
        ident_ready, block_ready = sem("ident_ready"), sem("block_ready")
        second_rest, second_part = sem("second_rest"), sem("second_part")

        block = ctx.enter_context(nc.Block())

        PRO = [("xnT", (k, tq)) for tq in range(NC) for k in range(KD)] + [("gate", 0)]
        PRO += [("proj", (s, 0, tc)) for s in range(2) for tc in range(NC)] + [("par", 0)]
        PRO += [("proj", (s, 1, tc)) for s in range(2) for tc in range(NC)]
        PRO += [("cum", 0)]
        PRO += [("feat", (s, tc, w)) for s in range(2) for tc in range(NC) for w in range(2)]
        PRO += [("v", n) for n in range(NT // 2)]
        READER = {"xnT": "act", "par": "dve", "gate": "dve", "proj": "act", "feat": "act", "cum": "dve", "v": "act"}
        PB = 5
        pro_act, pro_dve = sem("pro_act"), sem("pro_dve")
        reads = []
        for n, (kind, _) in enumerate(PRO):
            who = READER[kind]
            reads.append((pro_act if who == "act" else pro_dve, 1 + sum(READER[k] == who for k, _ in PRO[:n])))

        PAIRS = [(ic, 2 * p) for ic in range(NC) for p in range((ic + 1) * TC // 2)]
        NP = len(PAIRS)
        NSLOT = 4 * NP
        max0 = [("max2", (h,)) for h in range(GH)] + [("max", (h, it, 0)) for h in range(GH) for it in range(2, TC)]
        max1 = [("max", (h, it, pc)) for h in range(GH) for it in range(TC, NT) for pc in range(2)]

        def spread(tasks, first, last):
            return [(first + (last + 1 - first) * n // len(tasks), t) for n, t in enumerate(tasks)]

        def slotted(*lists):
            slots = [[] for _ in range(NSLOT)]
            for entries in lists:
                for at, t in entries:
                    slots[at].append(t)
            return slots
        EXPERT, SHARED = ("xT", "gu", "hT", "y"), ("gu", "hT", "y")
        own = [(1, ("oT", 1)), (9, ("oT", 0))]
        maxima = spread(max0, 4, 9) + [(11, ("shift", 0))] + spread(max1, 10, 21) + [(23, ("shift", 1))]
        PLAN1 = slotted(spread([(k, f) for f in range(EG) for k in EXPERT], 0, 22), own, maxima)
        shared = spread([(k, f) for f in range(SG) for k in SHARED], 2, 20)
        PLAN2 = {
            NH: slotted(own, maxima, shared, [(10, ("rows", (0, 0))), (14, ("rows", (0, 1)))]),
            NH + 1: slotted(own, maxima, shared, spread([("add", (k, n)) for n in range(TC) for k in range(2)], 3, 22)),
            NH + 2: slotted(own, maxima, shared, spread([("add", (k, n)) for n in range(TC, NT) for k in range(2)], 3, 22)),
            NH + 3: slotted(own, shared, [(6, ("out", (TC, 0))), (10, ("out", (TC + 2, 0))), (12, ("rows", (1, 0))),
                                          (15, ("out", (0, 2))), (18, ("out", (2, 2)))]),
        }
        END = [("oT", 1), ("rows", (1, 1)), ("out", (TC, 1)), ("out", (TC + 2, 1))]
        PRE = max0 + [("shift", 0)] + max1 + [("shift", 1)]
        AB = 3

        def banked(plan):
            return [t for slot in plan for t in slot if t[0] != "add"]
        NPRE, N1 = len(PRE), len(banked(PLAN1))
        assert NPRE % AB == 0 and N1 % AB == 0
        before2, at = {}, NPRE + NH * N1
        for g in range(NH, NG):
            before2[g] = at
            at += len(banked(PLAN2[g]))
        before2[NG] = at

        def place(g, task, phase):
            if phase == 0:
                n = PRE.index(task)
                return 5 + n % AB, n + 1
            if phase == 1:
                n = banked(PLAN1).index(task)
                return 5 + n % AB, g * N1 + (NPRE + n + 1)
            n = before2[g] + (END if g == NG else banked(PLAN2[g])).index(task)
            return 5 + n % AB, n + 1

        def shape_of(ic, jb):
            off = max(0, jb * P - ic * CH)
            return off, jb // TC == ic

        SPLIT_ORDER = [(0, 0), (1, 0), (2, 1), (2, 0), (3, 1), (3, 0), (0, 1), (1, 1)]

        def shape_of(ic, jb):
            off = max(0, jb * P - ic * CH)
            return off, jb // TC == ic

        @block.gpsimd
        def _(pool):
            steps = [0]

            def link(ins):
                steps[0] += 1
                ins.then_inc(pool_step, 1)
                pool.wait_ge(pool_step, steps[0])

            def select(t, op, fill, base, pattern, mult):
                return nc.gpsimd.affine_select(out=t, in_=t, compare_op=op, fill=fill, base=base,
                                               pattern=pattern, channel_multiplier=mult)
            nc.gpsimd.memset(blockm[:, :, :], 1.0)
            nc.gpsimd.memset(zero_i[:, :], 0)
            link(nc.gpsimd.memset(ident[:, :], 0.0))
            select(ident[:, :], ALU.not_equal, 1.0, 0, [[-1, P]], 1).then_inc(ident_ready, 1)
            pool.wait_ge(ident_ready, 1)
            for half in range(2):
                rows = blockm[64 * half:64 * half + 64, :, :]
                link(select(rows, ALU.is_ge, 0.0, 0, [[-NS, 8], [0, HD]], 1))
                ins = select(rows, ALU.is_ge, 0.0, NS - 1, [[NS, 8], [0, HD]], -1)
                ins.then_inc(block_ready, 1)
                pool.wait_ge(block_ready, half + 1)
            pool.dma_start(ids_d[0:DUMP, :].rearrange("(e c) o -> e (c o)", c=CAP), zero_i[:, :]).then_inc(ids0_out, 16)
            nc.gpsimd.iota(iota_i[:, :, :], [[T, 2], [P, NT]], base=DUMP, channel_multiplier=1)
            nc.gpsimd.iota(tok[:, :], [[P, NT]], base=0, channel_multiplier=1)
            nc.gpsimd.iota(iota_r[:, :, :], [[0, NT], [-1, E]], base=E, channel_multiplier=0,
                           allow_small_or_imprecise_dtypes=True)
            link(nc.gpsimd.iota(iota_s[:, :, :], [[0, NT], [CAP, E]], base=0, channel_multiplier=0,
                                allow_small_or_imprecise_dtypes=True))
            nc.gpsimd.tensor_copy(dump[:, :, :], iota_i[:, :, :])
            nc.gpsimd.memset(ident_b[:, :], 0.0)
            nc.gpsimd.memset(mask_t[:, :], 0.0)
            nc.gpsimd.memset(mask_n[:, :], 0.0)
            nc.gpsimd.memset(upper[:, :], 1.0)
            link(nc.gpsimd.memset(ones_b[:, :], 1.0))
            select(ident_b[:, :], ALU.not_equal, 1.0, 0, [[-1, P]], 1)
            select(mask_t[:, :], ALU.is_ge, NEG, 0, [[1, P]], -1)
            select(mask_n[:, :], ALU.is_ge, NEG, 0, [[-1, P]], 1)
            link(select(upper[:, :], ALU.is_gt, 0.0, 0, [[1, P]], -1))
            for n in range(4):
                link(nc.gpsimd.memset(stage[n][KR:KS, :, :, :], float(n % 2)))
            nc.gpsimd.memset(v_st[:, :, :, :, HD:], 1.0).then_inc(consts, 1)

            pool.wait_ge(ids0_out, 16)
            pool.wait_ge(slots_ready, 2)
            for k in range(2):
                for n in range(NT):
                    nc.gpsimd.indirect_dma_start(
                        out=ids_d[:, :], out_offset=bass.IndirectOffsetOnAxis(ap=sidx[:, k, n:n + 1], axis=0),
                        in_=tok[:, n:n + 1], in_offset=None).then_inc(ids_out, 16)
            pool.wait_ge(ids_out, 16 * 2 * NT)
            with nc.allow_non_contiguous_dma(reason="2,048 ids"):
                pool.dma_start(ids_sb[:, :], ids_d[0:DUMP, :].rearrange("(e c) o -> c (e o)", c=CAP)).then_inc(ids_in, 16)
            pool.wait_ge(ids_in, 16)
            pool.wait_ge(xn_out, 16)

            def values(g):
                src = v_all[:, :, bass.ds(g * (GH * HD), GH * HD)].rearrange("p n (h d) -> p n h d", h=GH)
                dst = v_st[:, bass.ds(g % 2, 1), :, :, 0:HD].rearrange("p o n h d -> p (o n) h d")
                nc.gpsimd.tensor_copy(dst, src).then_inc(v_ready, 1)

            def gather(g, f, first):
                if not first:
                    pool.wait_ge(aux_full, place(g - 1, ("xT", f), 1)[1])
                    pool.wait_ge(xe_in[f], 16 * g)
                nc.gpsimd.tensor_copy(ids_cur[:, f, :], ids_sb[:, bass.ds(g * EG + f, 1)]).then_inc(pool_ids, 1)
                pool.wait_ge(pool_ids, g * EG + (f + 1))
                pool.nop(nofuse=True)
                nc.gpsimd.indirect_dma_start(
                    out=xe[:, f, :], out_offset=None, in_=xn_d[:, :],
                    in_offset=bass.IndirectOffsetOnAxis(ap=ids_cur[:, f, :], axis=0)).then_inc(xe_in[f], 16)

            for f in range(EG):
                gather(0, f, True)
            pool.wait_ge(v_done, NT // 2)
            values(0)
            values(1)
            with pool.Fori(1, NH) as g:
                for f in range(EG):
                    gather(g, f, False)
                pool.wait_ge(acc_full, g * NC)
                values(g + 1)

            for f in range(EG):
                pool.wait_ge(ye_out[f], 16 * NH)
            for g in range(NH, NG - 1):
                for n in range({NH: NT}.get(g, 0)):
                    for k in range(2):
                        nc.gpsimd.indirect_dma_start(
                            out=gath[:, k, n, :], out_offset=None, in_=ye_d[:, :],
                            in_offset=bass.IndirectOffsetOnAxis(ap=gidx[:, k, n:n + 1], axis=0)).then_inc(gath_in[n], 16)
                    if n == 1:
                        pool.wait_ge(acc_full, g * NC)
                        values(g + 1)
                if g > NH:
                    pool.wait_ge(acc_full, g * NC)
                    values(g + 1)


        @block.sync
        def _(sp):
            w_v = wqkvo.rearrange("w (k p) d -> p w k d", p=P)
            for n in range(NC):
                sp.dma_start(acc[:, n * TC:(n + 1) * TC, :],
                             x[n * CH:(n + 1) * CH, :].rearrange("(n p) d -> p n d", p=P)).then_inc(x_in[n], 16)
            for w in range(2):
                sp.dma_start(wt[:, w, :, :], w_v[:, w, :, :]).then_inc(wqk_in, 16)
            for w in range(2, 4):
                sp.dma_start(wt[:, w, :, :], w_v[:, w, :, :]).then_inc(wvo_in, 16)
            sp.wait_ge(xn_ready, NT)
            sp.dma_start(xn_d.rearrange("(n p) d -> p n d", p=P), xn[:, :, :]).then_inc(xn_out, 16)
            def parts_to_dram(at):
                n, m = SPLIT_ORDER[at]
                sp.wait_ge(parts_ready, at + 1)
                for s in range(SPL):
                    slot = s if n % 2 == 0 else SPL - 1 - s
                    if n < 2:
                        dst = parts_d[n][m * NS:(m + 1) * NS, slot, :, :]
                    else:
                        dst = parts_d[n][:, slot, m * NS:(m + 1) * NS, :]
                    sp.dma_start(dst, split[:, n, s, m, :]).then_inc(parts_out[at], 16)

            def load_rows(g, pr, n, done):
                for row, qp, num, kp in RUNS:
                    part = qp if n % 2 == 0 else kp
                    src = parts_d[n][bass.ds(g * GH, GH), part:part + num, :, :].rearrange("h s r t -> (s r) h t")
                    sp.dma_start(stage[n][row * HD:(row + num) * HD, pr, :, :], src).then_inc(done[pr], 16)

            def load_qk(g, pr):
                load_rows(g, pr, 0, qk_in)
                load_rows(g, pr, 1, qk_in)

            def load_f(g, pr):
                load_rows(g, pr, 2, f_in)
                load_rows(g, pr, 3, f_in)

            def shift_rows(g, ic, pr, phase):
                sp.wait_ge(aux_free, place(g, ("shift", ic), phase)[1])
                for hl in range(2):
                    for h in range(GH):
                        row = (hl * GH + h) * TC
                        sp.dma_start(qs[KR + hl:KR + hl + 1, pr, h, ic * CH:(ic + 1) * CH],
                                     mT[row:row + TC, ic, :]).then_inc(shift_in[ic], 16)

            parts_to_dram(0)
            parts_to_dram(1)
            for at in range(2):
                sp.wait_ge(parts_out[at], 16 * SPL)
            sp.wait_ge(consts, 1)
            load_qk(0, 0)
            for f in range(EG):
                sp.dma_start(w13_sb[:, f, :, :], w13[f, :, :].rearrange("(k p) i -> p k i", p=P)).then_inc(w_in[f], 16)
                sp.dma_start(w2_sb[:, f, :, :], w2[f, :, :].rearrange("(k p) d -> p k d", p=I2)).then_inc(w_in[f], 16)
            for at in range(2, 6):
                parts_to_dram(at)
            for at in range(2, 6):
                sp.wait_ge(parts_out[at], 16 * SPL)
            load_f(0, 0)
            for ic in range(NC):
                shift_rows(-1, ic, 0, 0)
            for at in range(6, 8):
                parts_to_dram(at)
            for at in range(6, 8):
                sp.wait_ge(parts_out[at], 16 * SPL)

            def expert_out(g, f):
                sp.wait_ge(aux_free, place(g, ("y", f), 1)[1])
                sp.dma_start(ye_d[bass.ds((g * EG + f) * CAP, CAP), :], ye[:, f, :]).then_inc(ye_out[f], 16)

            def expert_in(g, f):
                sp.dma_start(w13_sb[:, f, :, :], w13[bass.ds(g * EG + f, 1), :, :]
                             .rearrange("o (k p) i -> p (o k) i", p=P)).then_inc(w_in[f], 16)
                sp.dma_start(w2_sb[:, f, :, :], w2[bass.ds(g * EG + f, 1), :, :]
                             .rearrange("o (k p) d -> p (o k) d", p=I2)).then_inc(w_in[f], 16)

            def body(g, pr, phase):
                if phase == 1 or g < NG - 1:
                    sp.wait_ge(acc_full, g * NC)
                    load_qk(g + 1, 1 - pr)
                    load_f(g + 1, 1 - pr)
                if phase == 1:
                    for f in range(EG):
                        expert_out(g, f)
                        if isinstance(g, int) and g == NH - 1:
                            if f == 0:
                                sp.dma_start(w13_sb[:, 0, :, :], ws13.rearrange("(k p) i -> p k i", p=P)).then_inc(ws_in, 16)
                                sp.dma_start(w2_sb[:, 0, :, :], ws2.rearrange("(k p) d -> p k d", p=I2)).then_inc(ws_in, 16)
                        else:
                            expert_in(g + 1, f)
                if phase == 1 or g < NG - 1:
                    for ic in range(NC):
                        shift_rows(g, ic, 1 - pr, phase)

            with sp.Fori(0, NH // 2 - 1) as it:
                body(it * 2, 0, 1)
                body(it * 2 + 1, 1, 1)
            body(NH - 2, 0, 1)
            body(NH - 1, 1, 1)
            for g in range(NH, NG):
                body(g, g % 2, 2)
            for g, n in ((NG - 1, 0), (NG - 1, 2), (NG, TC), (NG, TC + 2)):
                sp.wait_ge(aux_free, place(g, ("out", (n, 2 if n < TC else 1)), 2)[1])
                sp.dma_start(out[n * P:(n + 2) * P, :].rearrange("(n p) d -> p n d", p=P), acc[:, n:n + 2, :]).then_inc(y_out, 16)
            sp.wait_ge(y_out, 16 * 4)

        @block.scalar
        def _(act):
            A = nc.scalar.activation
            for dst, src in ((pos[:, :], positions), (dire[:, :], directions), (LS, log_scales), (LA, log_amplitudes)):
                act.dma_start(dst, src).then_inc(par_in, 16)
            for dst, src in ((PS, sensitivity), (DS, strength), (GG, gsa_gate)):
                act.dma_start(dst, src.to_broadcast((P, 1))).then_inc(par_in, 16)
            act.dma_start(gw_sb[:, :, :], gate_w.rearrange("(k p) e -> p k e", p=P)).then_inc(gate_in, 16)
            act.dma_start(gb_sb[:, 0, :], gate_b.to_broadcast((P, E))).then_inc(gate_in, 16)
            act.wait_ge(norm_ready, 1)
            A(NRM, NSQ, ACT.Sqrt).then_inc(norm_root, 1)
            act.wait_ge(var_ready, 1)
            A(vstd[:, 1, :], vstd[:, 0, :], ACT.Sqrt).then_inc(var_root, 1)

            def bank_ready(n):
                act.wait_ge(pro_full, n + 1)
                return ps[:, n % PB, :]

            def evacuate(n):
                kind, a = PRO[n]
                b = bank_ready(n)
                if kind == "xnT":
                    k, tq = a
                    A(xnT[:, k, tq * CH:(tq + 1) * CH], b, ACT.Copy).then_inc(pro_act, 1)
                elif kind == "proj":
                    s, m, tc = a
                    A(qkT[:, s, m, tc * CH:(tc + 1) * CH], b, ACT.Copy).then_inc(pro_act, 1)
                elif kind == "feat":
                    s, tc, w = a
                    A(feat[:, s, w, tc * CH:(tc + 1) * CH], b, ACT.Exp if w == 0 else ACT.Tanh,
                      bias=BG if w == 0 else BD).then_inc(pro_act, 1)
                else:
                    A(v_all[:, 2 * a:2 * a + 2, :].rearrange("p n d -> p (n d)"), b, ACT.Copy).then_inc(v_done, 1)

            def part0(at):
                n, m = SPLIT_ORDER[at]
                src = qkT[:, n, m, :] if n < 2 else feat[:, n - 2, m, :]
                if n < 2:
                    act.wait_ge(pro_act, reads[PRO.index(("proj", (n, m, 1)))][1])
                else:
                    act.wait_ge(features, n - 1)
                A(split[:, n, 0, m, :], src, ACT.Copy, scale=0.25 if n == 0 else 1.0).then_inc(first_part, 1)

            def part1(at):
                n, m = SPLIT_ORDER[at]
                act.wait_ge(second_rest, at + 1)
                A(split[:, n, 1, m, :], rest_[:, at % 2, :], ACT.Copy).then_inc(second_part, 1)

            tasks = [n for n, (k, _) in enumerate(PRO) if READER[k] == "act"]
            for n in tasks[:4]:
                evacuate(n)
            act.wait_ge(par_in, 16 * 7)
            A(IS2, LS, ACT.Exp, scale=-2.0)
            A(AMP, LA, ACT.Exp)
            A(EG_, GG, ACT.Exp, scale=-1.0).then_inc(par_exp, 1)
            act.wait_ge(gate_dve, 1)
            A(g_[2][:, :, :], g_[1][:, :, :], ACT.Exp, scale=-1.0).then_inc(gate_act, 1)
            evacuate(tasks[4])
            act.wait_ge(gate_dve, 2)
            A(g_[4][:, :, :], g_[3][:, :, :], ACT.Ln).then_inc(gate_act, 1)
            evacuate(tasks[5])
            act.wait_ge(gate_dve, 3)
            A(g_[10][:, :, :], g_[11][:, :, :], ACT.Sqrt).then_inc(gate_act, 1)
            evacuate(tasks[6])
            evacuate(tasks[7])
            part0(0)
            part0(1)
            for n in tasks[8:12]:
                evacuate(n)
            part1(0)
            part1(1)
            act.wait_ge(gw_ready, 1)
            for n in tasks[12:20]:
                evacuate(n)
            for at in range(2, 8, 2):
                part0(at)
                part0(at + 1)
                if at == 2:
                    for n in tasks[20:]:
                        evacuate(n)
                part1(at)
                part1(at + 1)

            act.wait_ge(parts_ready, 8)

            def body(g, plan, phase):
                for p, (ic, jb) in enumerate(PAIRS):
                    for turn in range(4):
                        var, s = divmod(turn, 2)
                        ready, done = (std_ready, std_exp) if var == 0 else (gsa_ready, gsa_exp)
                        off, _ = shape_of(ic, jb + s)
                        act.wait_ge(ready, g * (2 * NP) + (2 * p + s + 1))
                        A(probs[:, var, s, :, off:CH], ps[:, 1 + 2 * s:3 + 2 * s, off:CH], ACT.Exp).then_inc(done, 1)
                        for t in plan[4 * p + turn]:
                            if t[0] == "gu":
                                bank, count = place(g, t, phase)
                                act.wait_ge(aux_full, count)
                                A(th[:, :], ps[:, bank, 0:I], ACT.Tanh, scale=0.5).then_inc(th_ready, 1)

            with act.Fori(0, NH) as g:
                body(g, PLAN1, 1)
            for g in range(NH, NG):
                body(g, PLAN2[g], 2)

        @block.tensor
        def _(pe):
            M = nc.tensor.matmul
            pe.wait_ge(ident_ready, 1)

            def take(n):
                if n >= PB:
                    s, c = reads[n - PB]
                    if PRO[n - PB][0] == "v":
                        s = v_done
                    pe.wait_ge(s, c)
                return ps[:, n % PB, :]

            for n, (kind, a) in enumerate(PRO):
                b = take(n)
                if kind == "xnT":
                    k, tq = a
                    for i in range(TC):
                        t = tq * TC + i
                        pe.wait_ge(xn_ready, t + 1)
                        last = nc.tensor.transpose(b[:, i * P:(i + 1) * P], xn[:, t, k * P:(k + 1) * P], ident[:, :])
                elif kind == "par":
                    pe.wait_ge(gw_ready, 1)
                    for w in range(3):
                        last = nc.tensor.transpose(b[:, w * P:(w + 1) * P], gwide[:, w, :], ident[:, :])
                elif kind == "gate":
                    pe.wait_ge(gate_in, 32)
                    pe.wait_ge(pro_act, KD * NC)
                    for t in range(NT):
                        for k in range(KD):
                            last = M(b[:, t * E:(t + 1) * E], xnT[:, k, t * P:(t + 1) * P], gw_sb[:, k, :],
                                     start=k == 0, stop=k == KD - 1)
                elif kind == "proj":
                    s, m, tc = a
                    pe.wait_ge(wqk_in, 32)
                    for k in range(KD):
                        last = M(b, wt[:, s, k, m * P:(m + 1) * P], xnT[:, k, tc * CH:(tc + 1) * CH],
                                 start=k == 0, stop=k == KD - 1)
                elif kind == "feat":
                    s, tc, w = a
                    pe.wait_ge(pro_dve, 2)
                    pe.wait_ge(squares, 4)
                    for m in range(KD):
                        half = slice(64 * m, 64 * m + 64)
                        cols = slice(tc * CH, (tc + 1) * CH)
                        if w == 0:
                            M(b[half, :], gT[:, 0, half], sq[:, s, m, cols], start=True, stop=False)
                            last = M(b[half, :], gT[:, 1, half], qkT[:, s, m, cols], start=False, stop=True)
                        else:
                            last = M(b[half, :], gT[:, 2, half], qkT[:, s, m, cols], start=True, stop=True)
                elif kind == "cum":
                    pe.wait_ge(ohs_ready, 1)
                    pe.wait_ge(consts, 1)
                    M(b[:, 0:NT * E], upper[:, :], ohs[:, :, :].rearrange("p n e -> p (n e)"), start=True, stop=False)
                    for t in range(NT - 1):
                        rest = NT - 1 - t
                        last = M(b[:, (t + 1) * E:NT * E].rearrange("p (n e) -> p n e", e=E), ones_b[:, :],
                                 ohs[:, t:t + 1, :].to_broadcast((P, rest, E)), start=False, stop=t == NT - 2)
                else:
                    pe.wait_ge(wvo_in, 32)
                    for i in range(2):
                        for k in range(KD):
                            last = M(b[:, i * D:(i + 1) * D], xnT[:, k, (2 * a + i) * P:(2 * a + i + 1) * P],
                                     wt[:, 2, k, :], start=k == 0, stop=k == KD - 1)
                last.then_inc(pro_full, 1)

            def aux(g, t, phase, pr):
                kind, a = t
                if kind == "add":
                    return
                bank, count = place(g, t, phase)
                b = ps[:, bank, :]
                if not isinstance(count, int) or count > AB:
                    pe.wait_ge(aux_free, count - AB)
                if kind == "max2":
                    for it in range(2):
                        n0, n1 = it * P, it * 2 * P + P
                        M(b[:, n0:n1], qs[0:KR, pr, a[0], it * P:(it + 1) * P], ks[0:KR, pr, a[0], 0:(it + 1) * P],
                          start=True, stop=False)
                        ins = M(b[:, n1 - P:n1], ident_b[:, :], mask_n[:, :], start=False, stop=True)
                elif kind == "max":
                    h, it, pc = a
                    n0, n1 = pc * CH, min((it + 1) * P, (pc + 1) * CH)
                    diag = n1 == (it + 1) * P
                    lhs = qs[0:KR, pr, h, it * P:(it + 1) * P]
                    ins = M(b[:, 0:n1 - n0], lhs, ks[0:KR, pr, h, n0:n1], start=True, stop=not diag)
                    if diag:
                        ins = M(b[:, n1 - n0 - P:n1 - n0], ident_b[:, :], mask_n[:, :], start=False, stop=True)
                elif kind == "shift":
                    pe.wait_ge(mhl_ready, (g + 1) * NC + (a + 1))
                    ins = nc.tensor.transpose(psb[0:2 * GH * TC, bank, 0:P],
                                              mhl[:, a, :, :].rearrange("p s c -> p (s c)"), ident_b[:, :])
                elif kind == "xT":
                    pe.wait_ge(xe_in[a], (g + 1) * 16)
                    for k in range(KD):
                        ins = nc.tensor.transpose(b[:, k * P:(k + 1) * P], xe[:, a, k * P:(k + 1) * P], ident[:, :])
                elif kind == "gu":
                    if phase == 1:
                        pe.wait_ge(aux_free, place(g, ("xT", a), phase)[1])
                        pe.wait_ge(w_in[a], (g + 1) * 32)
                    else:
                        pe.wait_ge(ws_in, 32)
                    t0 = (g - NH) * SG + a if phase == 2 else 0
                    for k in range(KD):
                        lhs = xeT[:, k, :] if phase == 1 else xnT[:, k, t0 * P:(t0 + 1) * P]
                        ins = M(b[:, 0:2 * I], lhs, w13_sb[:, a if phase == 1 else 0, k, :], start=k == 0, stop=k == KD - 1)
                elif kind == "hT":
                    pe.wait_ge(aux_free, place(g, ("gu", a), phase)[1])
                    for c in range(2):
                        ins = nc.tensor.transpose(b[0:I2, c * P:(c + 1) * P], hh[:, c * I2:(c + 1) * I2], ident[:, :])
                elif kind == "y":
                    pe.wait_ge(aux_free, place(g, ("hT", a), phase)[1])
                    for c in range(2):
                        ins = M(b[:, 0:D], hT[:, c, :], w2_sb[:, a if phase == 1 else 0, c, :], start=c == 0, stop=c == 1)
                elif kind == "oT":
                    pe.wait_ge(acc_free, g * NC + (2 if a == 1 else 3))
                    for i in range(TC):
                        ins = nc.tensor.transpose(b[:, i * P:(i + 1) * P], pv_sb[:, i * P:(i + 1) * P], ident[:, :])
                elif kind == "rows":
                    k, tq = a
                    pe.wait_ge(o_ready, NH * NC + 1 if k == 0 else NG * NC + tq)
                    for i in range(TC):
                        ins = nc.tensor.transpose(b[:, i * P:(i + 1) * P], o_nat[:, tq * TC + i, GW + k * P:GW + (k + 1) * P], ident[:, :])
                else:
                    n, k = a
                    for rows in (("rows", (0, 0)), ("rows", (0, 1))) if k == 0 else (("rows", (1, 0 if n < TC else 1)),):
                        at = NH if k == 0 else NG - 1 if n < TC else NG
                        pe.wait_ge(aux_free, place(at, rows, 2)[1])
                    if k:
                        pe.wait_ge(aux_free, place(NH, ("rows", (0, 1)), 2)[1])
                    ks_ = (0, 1) if k == 2 else (k,)
                    for i in range(2):
                        for kk in ks_:
                            ins = M(b[:, i * D:(i + 1) * D], oT[:, kk, (n + i) * P:(n + i + 1) * P], wt[:, 3, kk, :],
                                    start=kk == ks_[0], stop=kk == ks_[-1])
                ins.then_inc(aux_full, 1)

            pe.wait_ge(consts, 1)
            pe.wait_ge(qk_in[0], 96)
            for t in PRE:
                aux(-1, t, 0, 0)

            def std(g, pr, p, s):
                ic, jb = PAIRS[p]
                off, diag = shape_of(ic, jb + s)
                if s == 0 and jb == 0:
                    pe.wait_ge(shift_in[ic], (g + 1) * 64)
                before = g * (2 * NP) + (2 * (p - 1) + s + 1)
                if not isinstance(before, int) or before > 0:
                    pe.wait_ge(gsa_exp, before)
                for h in range(GH):
                    b = ps[:, 1 + 2 * s + h, :]
                    ins = M(b[:, off:CH], ks[:, pr, h, (jb + s) * P:(jb + s + 1) * P],
                            qs[:, pr, h, ic * CH + off:(ic + 1) * CH], start=True, stop=not diag)
                    if diag:
                        ins = M(b[:, off:off + P], ident_b[:, :], mask_t[:, :], start=False, stop=True)
                ins.then_inc(std_ready, 1)

            def splat(g, pr, p, s):
                ic, jb = PAIRS[p]
                off, _ = shape_of(ic, jb + s)
                pe.wait_ge(std_exp, g * (2 * NP) + (2 * p + s + 1))
                for h in range(GH):
                    ins = M(ps[:, 1 + 2 * s + h, off:CH], fk[:, pr, h, (jb + s) * P:(jb + s + 1) * P],
                            fq[:, pr, h, ic * CH + off:(ic + 1) * CH], start=False, stop=True,
                            skip_group_check=True)
                ins.then_inc(gsa_ready, 1)

            def pv(g, pr, p, s):
                ic, jb = PAIRS[p]
                off, _ = shape_of(ic, jb + s)
                if jb + s == 0:
                    pe.wait_ge(acc_free, g * NC + (ic + 1))
                    pe.wait_ge(v_ready, g + 1)
                pe.wait_ge(gsa_exp, g * (2 * NP) + (2 * p + s + 1))
                end = jb + s == (ic + 1) * TC - 1
                for var in range(2):
                    for h in range(GH):
                        c = 2 * HD * (var * GH + h)
                        ins = M(ps[c:c + 2 * HD, 0, off:CH], v_st[:, pr, jb + s, h, :],
                                probs[:, var, s, h, off:CH], start=jb + s == 0, stop=end)
                if end:
                    ins.then_inc(acc_full, 1)

            def body(g, pr, plan, phase, half):
                nxt = half + pr
                last = phase == 2 and g == NG - 1

                def slot(n):
                    for t in plan[n]:
                        if t[0] in ("max", "max2"):
                            pe.wait_ge(qk_in[1 - pr], (nxt + 1) * 96)
                        aux(g, t, phase, 1 - pr)

                pe.wait_ge(f_in[pr], (half + 1) * 96)
                for p in range(NP):
                    slot(4 * p)
                    splat(g, pr, p, 0)
                    slot(4 * p + 1)
                    splat(g, pr, p, 1)
                    slot(4 * p + 2)
                    for s in range(2):
                        pv(g, pr, p, s)
                        if p + 1 < NP:
                            std(g, pr, p + 1, s)
                        elif not last:
                            if s == 0:
                                pe.wait_ge(qk_in[1 - pr], (nxt + 1) * 96)
                            std(g + 1, 1 - pr, 0, s)
                        if s == 0:
                            slot(4 * p + 3)

            pe.wait_ge(pro_act, reads[len(PRO) - NT // 2 - 1][1])
            pe.wait_ge(v_done, NT // 2)
            std(0, 0, 0, 0)
            std(0, 0, 0, 1)
            with pe.Fori(0, NH // 2) as it:
                body(it * 2, 0, PLAN1, 1, it)
                body(it * 2 + 1, 1, PLAN1, 1, it)
            for g in range(NH, NG):
                body(g, g % 2, PLAN2[g], 2, g // 2)
            for t in END:
                aux(NG, t, 2, 0)

        @block.vector
        def _(dve):
            V = nc.vector
            steps, base = [0], [0]

            def link(ins):
                steps[0] += 1
                ins.then_inc(dve_step, 1)
                dve.wait_ge(dve_step, base[0] + steps[0])

            def tt(out, a, b, op):
                return V.tensor_tensor(out, a, b, op)

            dve.wait_ge(par_in, 16 * 7)
            tt(tmp16[:, 0, :], dire[:, :], dire[:, :], ALU.mult)
            link(tt(tmp16[:, 1, :], pos[:, :], pos[:, :], ALU.mult))
            V.reduce_sum(PP, tmp16[:, 1, :], AX.X)
            V.reduce_sum(NSQ, tmp16[:, 0, :], AX.X).then_inc(norm_ready, 1)
            for t in range(NT):
                dve.wait_ge(x_in[t // TC], 16)
                ins = V.bn_stats(stats[:, t, :], acc[:, t, :])
            link(ins)
            for t in range(NT):
                ins = V.bn_aggr(mv[:, t, :], stats[:, t, :])
            link(ins)
            V.tensor_scalar(vstd[:, 0, :], mv[:, :, 1], EPS, None, ALU.add).then_inc(var_ready, 1)
            dve.wait_ge(var_root, 1)
            link(V.reciprocal(vstd[:, 0, :], vstd[:, 1, :]))
            for t in range(NT):
                V.tensor_scalar(xn[:, t, :], acc[:, t, :], mv[:, t, 0:1], vstd[:, 0, t:t + 1],
                                ALU.subtract, ALU.mult).then_inc(xn_ready, 1)
            dve.wait_ge(norm_root, 1)
            dve.wait_ge(par_exp, 1)
            dve.wait_ge(block_ready, 2)
            link(V.tensor_scalar(TMP, NRM, 1e-8, None, ALU.add))
            link(V.reciprocal(RN, TMP))
            V.tensor_scalar(HI2, IS2, -0.5, None, ALU.mult)
            V.tensor_scalar(tmp16[:, 3, :], pos[:, :], IS2, None, ALU.mult)
            V.tensor_scalar(C1, AMP, PS, None, ALU.mult)
            V.tensor_scalar(B1_, EG_, 1.0, None, ALU.add)
            link(V.tensor_scalar(tmp16[:, 2, :], dire[:, :], RN, None, ALU.mult))
            V.tensor_scalar(C2, C1, DS, None, ALU.mult)
            V.tensor_scalar(BG, HI2, PP, None, ALU.mult)
            V.reciprocal(B_, B1_)
            V.tensor_scalar(gwide[:, 0, :], blockm[:, :, :].rearrange("p h d -> p (h d)"), HI2, None, ALU.mult)
            tt(gwide[:, 1, :].rearrange("p (h d) -> p h d", d=HD), blockm[:, :, :],
               tmp16[:, 3:4, :].to_broadcast((P, NS, HD)), ALU.mult)
            tt(gwide[:, 2, :].rearrange("p (h d) -> p h d", d=HD), blockm[:, :, :],
               tmp16[:, 2:3, :].to_broadcast((P, NS, HD)), ALU.mult)
            link(tt(tmp16[:, 0, :], pos[:, :], tmp16[:, 2, :], ALU.mult))
            V.tensor_scalar(blendw[:, 2:3], B_, 0.15, 0.03, ALU.mult, ALU.min)
            link(V.reduce_sum(PD, tmp16[:, 0, :], AX.X))
            V.tensor_scalar(blendw[:, 3:4], blendw[:, 2:3], 1.0, None, ALU.mult)
            V.tensor_scalar(blendw[:, 0:1], blendw[:, 2:3], -1.0, 1.0, ALU.mult, ALU.add)
            V.tensor_scalar(blendw[:, 1:2], blendw[:, 2:3], -1.0, 1.0, ALU.mult, ALU.add)
            V.tensor_scalar(BD, PD, -1.0, None, ALU.mult).then_inc(gw_ready, 1)
            n = PRO.index(("gate", 0))
            dve.wait_ge(pro_full, n + 1)
            flat = ps[:, n % PB, 0:NT * E].rearrange("p (n e) -> p n e", e=E)
            G = [g[:, :, :] for g in g_]
            R = [r_[:, n, :] for n in range(16)]

            def row(r):
                return r.unsqueeze(2).to_broadcast((P, NT, E))
            V.tensor_copy(G[0], flat).then_inc(pro_dve, 1)
            dve.wait_ge(pro_dve, 1)
            V.scalar_tensor_tensor(out=G[1], in0=G[0], scalar=-1.0, in1=G[0], op0=ALU.mult, op1=ALU.max).then_inc(gate_dve, 1)
            V.tensor_scalar(G[5], G[0], 0.0, None, ALU.max)
            dve.wait_ge(gate_act, 1)
            V.tensor_scalar(G[3], G[2], 1.0, None, ALU.add).then_inc(gate_dve, 1)
            dve.wait_ge(gate_dve, 2)
            link(V.tensor_scalar(G[6], G[3], -1.0, None, ALU.add))
            link(V.tensor_scalar(G[7], G[6], 0.0, None, ALU.is_equal))
            link(tt(G[6], G[6], G[7], ALU.add))
            V.reciprocal(G[8], G[6])
            link(tt(G[9], G[7], G[2], ALU.mult))
            link(tt(G[8], G[8], G[2], ALU.mult))
            dve.wait_ge(gate_act, 2)
            link(tt(G[8], G[8], G[4], ALU.mult))
            link(tt(G[8], G[8], G[9], ALU.add))
            tt(G[11], G[8], G[5], ALU.add).then_inc(gate_dve, 1)
            dve.wait_ge(gate_act, 3)
            link(tt(G[11], G[10], gb_sb[:, :, :].to_broadcast((P, NT, E)), ALU.add))
            choose, score, oh = G[11], G[10], [G[2], G[5]]
            dve.wait_ge(consts, 1)
            for k in range(2):
                link(V.reduce_max(R[0], choose, AX.X))
                link(tt(G[1], choose, row(R[0]), ALU.is_ge))
                link(tt(G[1], G[1], iota_r[:, :, :], ALU.mult))
                link(V.reduce_max(R[1], G[1], AX.X))
                link(tt(oh[k], G[1], row(R[1]), ALU.is_equal))
                if k == 0:
                    link(V.scalar_tensor_tensor(out=choose, in0=oh[0], scalar=NEG, in1=choose, op0=ALU.mult, op1=ALU.add))
                link(tt(G[1], oh[k], score, ALU.mult))
                link(V.reduce_sum(R[2 + k], G[1], AX.X))
            tt(ohs[:, :, :], oh[0], oh[1], ALU.add).then_inc(ohs_ready, 1)
            link(tt(R[4], R[2], R[3], ALU.add))
            link(V.reciprocal(R[5], R[4]))

            def slots():
                n = PRO.index(("cum", 0))
                dve.wait_ge(pro_full, n + 1)
                V.tensor_copy(G[7], ps[:, n % PB, 0:NT * E].rearrange("p (n e) -> p n e", e=E)).then_inc(pro_dve, 1)
                dve.wait_ge(pro_dve, 3)
                link(tt(G[8], G[7], iota_s[:, :, :], ALU.add))
                for k in range(2):
                    tt(G[9], oh[k], G[7], ALU.mult)
                    link(tt(G[1], oh[k], G[8], ALU.mult))
                    V.reduce_sum(R[6], G[9], AX.X)
                    link(V.reduce_sum(R[7], G[1], AX.X))
                    link(V.tensor_scalar(R[8], R[6], float(CAP), None, ALU.is_lt))
                    tt(R[9], R[2 + k], R[5], ALU.mult)
                    tt(R[10], R[7], R[8], ALU.mult)
                    link(tt(R[11], R[7], dump[:, k, :], ALU.subtract))
                    tt(pairw[:, k, :], R[9], R[8], ALU.mult)
                    V.tensor_copy(gidx[:, k, :], R[10])
                    link(tt(R[12], R[11], R[8], ALU.mult))
                    link(tt(R[13], R[12], dump[:, k, :], ALU.add))
                    V.tensor_copy(sidx[:, k, :], R[13]).then_inc(slots_ready, 1)

            def part_pair(at0):
                for at in (at0, at0 + 1):
                    n, m = SPLIT_ORDER[at]
                    src = qkT[:, n, m, :] if n < 2 else feat[:, n - 2, m, :]
                    dve.wait_ge(first_part, at + 1)
                    if at >= 2:
                        dve.wait_ge(parts_ready, at - 1)
                    V.scalar_tensor_tensor(out=rest_[:, at % 2, :], in0=src, scalar=0.25 if n == 0 else 1.0,
                                           in1=split[:, n, 0, m, :], op0=ALU.mult, op1=ALU.subtract).then_inc(second_rest, 1)
                for at in (at0, at0 + 1):
                    n, m = SPLIT_ORDER[at]
                    dve.wait_ge(second_rest, at + 1)
                    dve.wait_ge(second_part, at + 1)
                    tt(split[:, n, 2, m, :], rest_[:, at % 2, :], split[:, n, 1, m, :], ALU.subtract).then_inc(parts_ready, 1)

            n = PRO.index(("par", 0))
            dve.wait_ge(pro_full, n + 1)
            V.tensor_copy(gT[:, :, :].rearrange("p w c -> p (w c)"), ps[:, n % PB, 0:3 * P]).then_inc(pro_dve, 1)
            part_pair(0)
            for s in range(2):
                for m in range(KD):
                    dve.wait_ge(pro_act, reads[PRO.index(("proj", (s, m, 1)))][1])
                    tt(sq[:, s, m, :], qkT[:, s, m, :], qkT[:, s, m, :], ALU.mult).then_inc(squares, 1)
            slots()
            for s in range(2):
                dve.wait_ge(pro_act, reads[PRO.index(("feat", (s, 1, 1)))][1])
                gs, dr = feat[:, s, 0, :], feat[:, s, 1, :]
                if s == 0:
                    link(V.scalar_tensor_tensor(out=dr, in0=gs, scalar=C2, in1=dr, op0=ALU.mult, op1=ALU.mult))
                    V.tensor_scalar(gs, gs, C1, None, ALU.mult).then_inc(features, 1)
                else:
                    tt(dr, gs, dr, ALU.mult).then_inc(features, 1)
            for at0 in range(2, 8, 2):
                part_pair(at0)
            V.memset(mx[:, :, :, :, :], 0.0).then_inc(acc_free, 1)
            dve.wait_ge(acc_free, 1)

            def aux(g, t, phase):
                kind, a = t
                if kind == "add":
                    k, n = a
                    dve.wait_ge(gath_in[n], 32)
                    link(V.scalar_tensor_tensor(out=acc[:, n, :], in0=gath[:, k, n, :], scalar=pairw[:, k, n:n + 1],
                                                in1=acc[:, n, :], op0=ALU.mult, op1=ALU.add))
                    return
                bank, count = place(g, t, phase)
                b = ps[:, bank, :]
                dve.wait_ge(aux_full, count)
                if kind == "max2":
                    V.reduce_max(mx[:, 0, a[0], 0, 0:1], b[:, 0:P], AX.X)
                    V.reduce_max(mx[:, 0, a[0], 1, 0:1], b[:, P:3 * P], AX.X).then_inc(aux_free, 1)
                elif kind == "max":
                    h, it, pc = a
                    n0, n1 = pc * CH, min((it + 1) * P, (pc + 1) * CH)
                    V.reduce_max(mx[:, it // TC, h, it % TC, pc:pc + 1], b[:, 0:n1 - n0], AX.X).then_inc(aux_free, 1)
                    if t == max0[-1] or t == max1[-1]:
                        ic = it // TC
                        dve.wait_ge(aux_free, count)
                        if ic == 0:
                            link(V.tensor_scalar(mneg[:, 0, :, :], mx[:, 0, :, :, 0], -1.0, None, ALU.mult))
                        else:
                            link(tt(mneg[:, 1, :, :], mx[:, 1, :, :, 0], mx[:, 1, :, :, 1], ALU.max))
                            link(V.tensor_scalar(mneg[:, 0, :, :], mneg[:, 1, :, :], -1.0, None, ALU.mult))
                        m32 = mneg[:, 0, :, :].rearrange("p h n -> p (h n)")
                        link(V.tensor_copy(mhl[:, ic, 0, :], m32))
                        tt(mhl[:, ic, 1, :], m32, mhl[:, ic, 0, :], ALU.subtract).then_inc(mhl_ready, 1)
                elif kind == "shift":
                    if phase:
                        dve.wait_ge(shift_in[a], (g + 1) * 64)
                    V.tensor_copy(mT[:, a, :], psb[0:2 * GH * TC, bank, 0:P]).then_inc(aux_free, 1)
                elif kind == "xT":
                    V.tensor_copy(xeT[:, :, :].rearrange("p k c -> p (k c)"), b[:, 0:D]).then_inc(aux_free, 1)
                elif kind == "gu":
                    first = g * EG + (a + 1) if phase == 1 else NH * EG + (g - NH) * SG + a + 1
                    dve.wait_ge(th_ready, first)
                    link(V.scalar_tensor_tensor(out=h1[:, :], in0=th[:, :], scalar=1.0, in1=b[:, 0:I], op0=ALU.add, op1=ALU.mult))
                    V.scalar_tensor_tensor(out=hh[:, :], in0=h1[:, :], scalar=0.5, in1=b[:, I:2 * I],
                                           op0=ALU.mult, op1=ALU.mult).then_inc(aux_free, 1)
                elif kind == "hT":
                    V.tensor_copy(hT[:, :, :].rearrange("p k c -> p (k c)"), b[0:I2, 0:2 * P]).then_inc(aux_free, 1)
                elif kind == "y":
                    if phase == 1:
                        dve.wait_ge(ye_out[a], g * 16)
                        V.tensor_copy(ye[:, a, :], b[:, 0:D]).then_inc(aux_free, 1)
                    else:
                        dst = acc[:, (g - NH) * SG + a, :]
                        tt(dst, b[:, 0:D], dst, ALU.add).then_inc(aux_free, 1)
                        dve.wait_ge(aux_free, count)
                elif kind == "oT":
                    o4 = b[:, :].rearrange("p (n v c) -> p n v c", n=TC, v=4)
                    link(V.reciprocal(rec[:, :, :], o4[:, :, :, HD]))
                    link(tt(recw[:, :, :], rec[:, :, :], blendw[:, :].unsqueeze(1).to_broadcast((P, TC, 4)), ALU.mult))
                    tt(onv[:, :, :, :], o4[:, :, :, 0:HD], recw[:, :, :].unsqueeze(3).to_broadcast((P, TC, 4, HD)), ALU.mult).then_inc(aux_free, 1)
                    dve.wait_ge(aux_free, count)
                    col = g * GW if a == 1 else g * GW + GW
                    dst = o_nat[:, a * TC:(a + 1) * TC, bass.ds(col, GW)].rearrange("p n (h d) -> p n h d", h=GH)
                    tt(dst, onv[:, :, 0:2, :], onv[:, :, 2:4, :], ALU.add).then_inc(o_ready, 1)
                elif kind == "rows":
                    k, tq = a
                    V.tensor_copy(oT[:, k, tq * CH:(tq + 1) * CH], b).then_inc(aux_free, 1)
                else:
                    n, k = a
                    dst = acc[:, n:n + 2, :].rearrange("p n d -> p (n d)")
                    tt(dst, b, dst, ALU.add).then_inc(aux_free, 1)
                    dve.wait_ge(aux_free, count)

            def evac(g, ic):
                dve.wait_ge(acc_full, g * NC if ic == 1 else g * NC + 1)
                V.tensor_copy(pv_sb[:, :], ps[:, 0, :]).then_inc(acc_free, 1)

            for t in PRE:
                aux(-1, t, 0)
            V.memset(ps[:, 0, :], 1.0).then_inc(acc_one, 1)
            dve.wait_ge(acc_one, 1)

            def body(g, plan, phase):
                for n in range(NSLOT):
                    if n == 0:
                        evac(g, 1)
                    if n == 8:
                        evac(g, 0)
                    for t in plan[n]:
                        aux(g, t, phase)

            LINKS0 = steps[0]
            LINKS = sum({"gu": 1, "oT": 2}.get(t[0], 0) + (2 if t == max0[-1] else 3 if t == max1[-1] else 0) for t in banked(PLAN1))
            with dve.Fori(0, NH) as g:
                base[0], steps[0] = LINKS * g, LINKS0
                body(g, PLAN1, 1)
            assert steps[0] == LINKS0 + LINKS
            base[0] = LINKS * (NH - 1)
            for g in range(NH, NG):
                body(g, PLAN2[g], 2)
            evac(NG, 1)
            for t in END:
                aux(NG, t, 2)

    return nc


_INS = ["x", "wqkvo", "positions", "directions", "log_scales", "log_amplitudes", "strength", "sensitivity",
        "gsa_gate", "gate_w", "gate_b", "w13", "w2", "ws13", "ws2"]


def kernel(**inputs):
    import numpy as np
    import concourse.bacc as bacc
    from concourse import mybir as mb
    from concourse.bass_utils import run_bass_kernel_spmd as run

    def a(name):
        return np.asarray(inputs[name])

    def c(v):
        return np.ascontiguousarray(v)

    x = a("L0_attn_hidden_states")
    w = [a("L0_attn_" + n) for n in ("Wq", "Wk", "Wv", "Wo")]
    W1, W3, W2 = a("L0_ffn_W1"), a("L0_ffn_W3"), a("L0_ffn_W2")
    laid = {
        "x": x.reshape(x.shape[1], x.shape[2]),
        "wqkvo": np.stack([m.T for m in w]),
        "positions": a("L0_attn_splat_positions").reshape(128, 16),
        "directions": a("L0_attn_splat_directions").reshape(128, 16),
        "log_scales": a("L0_attn_splat_log_scales").reshape(128, 1),
        "log_amplitudes": a("L0_attn_splat_log_amplitudes").reshape(128, 1),
        "strength": a("L0_attn_directional_strength").reshape(1, 1),
        "sensitivity": a("L0_attn_position_sensitivity").reshape(1, 1),
        "gsa_gate": a("L0_attn_gsa_strength").reshape(1, 1),
        "gate_w": a("L0_ffn_gate_w").T,
        "gate_b": a("L0_ffn_gate_b").reshape(1, -1),
        "w13": np.concatenate([W1.transpose(0, 2, 1), W3.transpose(0, 2, 1)], axis=2),
        "w2": W2.transpose(0, 2, 1),
        "ws13": np.concatenate([a("L0_ffn_Ws1").T, a("L0_ffn_Ws3").T], axis=1),
        "ws2": a("L0_ffn_Ws2").T,
    }
    nc = bacc.Bacc("TRN2", target_bir_lowering=False, num_devices=1)
    arrays, args = {}, []
    for name in _INS:
        v = c(laid[name])
        arrays[f"in_{name}_dram"] = v
        args.append(nc.dram_tensor(f"in_{name}_dram", v.shape, mb.dt.from_np(v.dtype), kind="ExternalInput").ap())
    out = nc.dram_tensor("out_dram", (x.shape[1], x.shape[2]), mb.dt.from_np(x.dtype), kind="ExternalOutput").ap()
    bass_splat_attention_moe_layer(nc, *args, out)
    r = run(nc, [arrays], core_ids=[0])
    return r.results[0]["out_dram"].reshape(x.shape)
```

```python
from contextlib import ExitStack

import concourse.bass as bass
from concourse import mybir


def bass_splat_attention_moe_layer(nc, x, wqkvo, positions, directions, log_scales, log_amplitudes,
                                   strength, sensitivity, gsa_gate, gate_w, gate_b,
                                   w13, w2, ws13, ws2, out):
    f32, bf16, u32 = mybir.dt.float32, mybir.dt.bfloat16, mybir.dt.uint32
    ALU, ACT, AX = mybir.AluOpType, mybir.ActivationFunctionType, mybir.AxisListType

    T, D = x.shape
    P = 128
    NT = T // P
    KD = D // P
    H, NS, HD = 16, 8, 16
    E, I, CAP = 16, 176, 128
    I2 = I // 2
    CH = 512
    NC = T // CH
    TC = CH // P
    GH = 2
    NG = H // GH
    NH = NG // 2
    EG = E // NH
    SG = NT // NH
    SPL = 3
    RUNS = [(0, 0, 3, 0), (3, 0, 2, 1), (5, 0, 1, 2)]
    KR = HD * 6
    KS = KR + 2
    NEG = -1.0e30
    DUMP = E * CAP
    EPS = 1e-5
    SAFE = 40.0

    xn_d = nc.dram_tensor("xn_scratch", (T, D), f32).ap()
    ids_d = nc.dram_tensor("ids_scratch", (DUMP + 2 * T, 1), u32).ap()
    ye_d = nc.dram_tensor("ye_scratch", (E * CAP, D), f32).ap()
    parts_d = [nc.dram_tensor(f"parts_scratch{n}", (H, SPL, HD, T), bf16).ap() for n in range(4)]

    gap_d = nc.dram_tensor("gap_scratch", (NG, 2, GH, T), bf16).ap()

    ctx = ExitStack()
    with ctx:
        def sb(name, shape, dt):
            return ctx.enter_context(nc.sbuf_tensor(name, shape, dt))

        def sem(name):
            return ctx.enter_context(nc.semaphore(name))

        acc = sb("acc", [P, NT, D], f32)
        xn = sb("xn", [P, NT, D], f32)
        xnT = sb("xnT", [P, KD, T], f32)
        wt = sb("wt", [P, 4, KD, D], f32)
        v_all = sb("v_all", [P, NT, D], f32)
        v_st = sb("v_st", [P, 2, NT, GH, 2 * HD], f32)
        stage = [sb(f"stage{n}", [KS, 2, GH, T], bf16) for n in range(4)]
        qs, ks, fq, fk = stage
        arena_p = sb("arena_p", [P, 4, 1024], f32)
        arena_o = sb("arena_o", [P, 4, T], f32)
        rest_ = sb("rest", [P, 2, T], f32)
        split = sb("split", [P, 4, SPL, 2, T], bf16)
        sq = [split[:, 2 + s, :, :, :].rearrange("p b c t -> p (b c t)").bitcast(f32)[:, 0:KD * T]
              .rearrange("p (m t) -> p m t", m=KD) for s in range(2)]
        qkT = arena_p[:, :, :].rearrange("p (s m) t -> p s m t", s=2)
        feat = arena_o[:, :, :].rearrange("p (s m) t -> p s m t", s=2)
        probs = arena_p[:, :, :].rearrange("p (v s) (h n) -> p v s h n", v=2, h=GH)
        GW = GH * HD
        o_nat = arena_o[:, :, :].rearrange("p a t -> p (a t)")[:, 0:NT * (D + GW)].rearrange("p (n d) -> p n d", d=D + GW)
        oT = rest_
        gath = split[:, :, :, :, :].rearrange("p a b c t -> p (a b c t)").bitcast(f32)[:, 0:2 * NT * D] \
            .rearrange("p (k n d) -> p k n d", k=2, n=NT)

        w13_sb = sb("w13_sb", [P, EG, KD, 2 * I], f32)
        w2_sb = sb("w2_sb", [I2, EG, 2, D], f32)
        xe = sb("xe", [P, EG, D], f32)
        xeT = sb("xeT", [P, KD, P], f32)
        th = sb("th", [P, I], f32)
        h1 = sb("h1", [P, I], f32)
        hh = sb("hh", [P, I], f32)
        hT = sb("hT", [I2, 2, P], f32)
        ye = sb("ye", [P, EG, D], f32)
        pv_sb = sb("pv_sb", [P, CH], f32)
        rec = sb("rec", [P, TC, 4], f32)
        recw = sb("recw", [P, TC, 4], f32)
        onv = sb("onv", [P, TC, 4, HD], f32)
        mx = sb("mx", [P, 2, GH, TC, 2], f32)
        mneg = sb("mneg", [P, 2, GH, TC], f32)
        mhl = sb("mhl", [P, 2, 2, GH * TC], bf16)
        mT = sb("mT", [2 * GH * TC, 2, P], bf16)

        ident = sb("ident", [P, P], f32)
        ident_b = sb("ident_b", [P, P], bf16)
        mask_t = sb("mask_t", [P, P], bf16)
        mask_n = sb("mask_n", [P, P], bf16)
        upper = sb("upper", [P, P], bf16)
        ones_b = sb("ones_b", [P, P], bf16)
        blockm = sb("blockm", [P, NS, HD], f32)
        iota_r = sb("iota_r", [P, NT, E], f32)
        iota_s = sb("iota_s", [P, NT, E], f32)
        iota_i = sb("iota_i", [P, 2, NT], u32)
        tok = sb("tok", [P, NT], u32)
        dump = sb("dump", [P, 2, NT], f32)
        zero_i = sb("zero_i", [E, CAP], u32)

        pos = sb("pos", [P, HD], f32)
        dire = sb("dire", [P, HD], f32)
        par = sb("par", [P, 26], f32)
        (LS, LA, PS, DS, GG, IS2, AMP, NSQ, NRM, RN, PD, PP, BG, C1, C2, BD, HI2, EG_, B_, B1_, TMP, AC, AD, BND) = \
            [par[:, n:n + 1] for n in range(24)]
        bound = sb("bound", [1, H + 1], f32)
        wide = sb("wide", [1, 1], u32)
        own_mx = sb("own_mx", [P, 3, GH, NT], f32)
        own_hl = sb("own_hl", [P, 2, GH, NT], bf16)
        own_T = sb("own_T", [2 * GH * NT, P], bf16)
        tmp16 = sb("tmp16", [P, 4, HD], f32)
        gwide = pv_sb[:, 0:3 * P].rearrange("p (w c) -> p w c", w=3)
        gT = sb("gT", [P, 3, P], f32)
        blendw = sb("blendw", [P, 4], f32)
        stats = sb("stats", [P, NT, 6], f32)
        mv = sb("mv", [P, NT, 2], f32)
        vstd = sb("vstd", [P, 2, NT], f32)
        gw_sb = sb("gw_sb", [P, KD, E], f32)
        gb_sb = sb("gb_sb", [P, 1, E], f32)
        g_ = [v_all[:, n // 2, (n % 2) * P:(n % 2 + 1) * P].rearrange("p (n e) -> p n e", e=E) for n in range(12)]
        ohs = sb("ohs", [P, NT, E], bf16)
        r_ = sb("r_", [P, 16, NT], f32)
        sidx = sb("sidx", [P, 2, NT], u32)
        gidx = sb("gidx", [P, 2, NT], u32)
        pairw = sb("pairw", [P, 2, NT], f32)
        ids_sb = sb("ids_sb", [P, E], u32)
        ids_cur = sb("ids_cur", [P, EG, 1], u32)

        ps = ctx.enter_context(nc.psum_tensor("ps", [P, 8, CH], f32))
        psb = ps[:, :, :].rearrange("p b n -> p (b n)").bitcast(bf16).rearrange("p (b n) -> p b n", b=8)

        par_in, wqk_in, wvo_in, gate_in, ws_in = (sem(n) for n in ("par_in", "wqk_in", "wvo_in", "gate_in", "ws_in"))
        consts = sem("consts")
        dve_step, pool_step = sem("dve_step"), sem("pool_step")
        x_in = [sem(f"x_in{n}") for n in range(NC)]
        pool_ids = sem("pool_ids")
        norm_ready, norm_root, var_ready, var_root = sem("norm_ready"), sem("norm_root"), sem("var_ready"), sem("var_root")
        xn_ready, par_exp, gw_ready, gate_dve, gate_act = (sem(n) for n in ("xn_ready", "par_exp", "gw_ready", "gate_dve", "gate_act"))
        ohs_ready, slots_ready, v_done = sem("ohs_ready"), sem("slots_ready"), sem("v_done")
        first_part, squares, features, parts_ready = sem("first_part"), sem("squares"), sem("features"), sem("parts_ready")
        pro_full = sem("pro_full")
        xn_out, ids0_out, ids_out, ids_in = sem("xn_out"), sem("ids0_out"), sem("ids_out"), sem("ids_in")
        parts_out = [sem(f"parts_out{n}") for n in range(8)]
        qk_in = [sem(f"qk_in{n}") for n in range(2)]
        f_in = [sem(f"f_in{n}") for n in range(2)]
        aux_full, aux_free = sem("aux_full"), sem("aux_free")
        std_ready, std_exp, gsa_ready, gsa_exp = sem("std_ready"), sem("std_exp"), sem("gsa_ready"), sem("gsa_exp")
        acc_full, acc_free, acc_one = sem("acc_full"), sem("acc_free"), sem("acc_one")
        o_ready = sem("o_ready")
        shift_in = [sem(f"shift_in{n}") for n in range(NC)]
        v_ready, mhl_ready = sem("v_ready"), sem("mhl_ready")
        xe_in = [sem(f"xe_in{n}") for n in range(EG)]
        w_in = [sem(f"w_in{n}") for n in range(EG)]
        th_ready = sem("th_ready")
        ye_out = [sem(f"ye_out{n}") for n in range(EG)]
        gath_in = [sem(f"gath_in{n}") for n in range(NT)]
        y_out = sem("y_out")
        ident_ready, block_ready = sem("ident_ready"), sem("block_ready")
        second_rest, second_part = sem("second_rest"), sem("second_part")
        zeros_out, wide_ready = sem("zeros_out"), sem("wide_ready")
        own_in, own_plain, own_plain_read, own_full, own_read = (
            sem(n) for n in ("own_in", "own_plain", "own_plain_read", "own_full", "own_read"))
        own_step = sem("own_step")
        own_split, own_turned, own_rows, own_out = (sem(n) for n in ("own_split", "own_turned", "own_rows", "own_out"))

        block = ctx.enter_context(nc.Block())

        PRO = [("xnT", (k, tq)) for tq in range(NC) for k in range(KD)]
        PRO += [("proj", (0, 0, tc)) for tc in range(NC)] + [("gate", 0)]
        PRO += [("proj", (1, 0, tc)) for tc in range(NC)] + [("par", 0)]
        PRO += [("proj", (s, 1, tc)) for s in range(2) for tc in range(NC)]
        PRO += [("feat", (0, tc, w)) for tc in range(NC) for w in range(2)]
        PRO += [("cum", 0)]
        PRO += [("feat", (1, tc, w)) for tc in range(NC) for w in range(2)]
        PRO += [("v", n) for n in range(NT // 2)]
        READER = {"xnT": "act", "par": "dve", "gate": "dve", "proj": "act", "feat": "act", "cum": "dve", "v": "act"}
        PB = 5
        pro_act, pro_dve = sem("pro_act"), sem("pro_dve")
        reads = []
        for n, (kind, _) in enumerate(PRO):
            who = READER[kind]
            reads.append((pro_act if who == "act" else pro_dve, 1 + sum(READER[k] == who for k, _ in PRO[:n])))

        PAIRS = [(ic, 2 * p) for ic in range(NC) for p in range((ic + 1) * TC // 2)]
        NP = len(PAIRS)
        NSLOT = 4 * NP
        max0 = [("max2", (h,)) for h in range(GH)] + [("max", (h, it, 0)) for h in range(GH) for it in range(2, TC)]
        max1 = [("max", (h, it, pc)) for h in range(GH) for it in range(TC, NT) for pc in range(2)]

        def spread(tasks, first, last):
            return [(first + (last + 1 - first) * n // len(tasks), t) for n, t in enumerate(tasks)]

        def slotted(*lists):
            slots = [[] for _ in range(NSLOT)]
            for entries in lists:
                for at, t in entries:
                    slots[at].append(t)
            return slots
        EXPERT, SHARED = ("xT", "gu", "hT", "y"), ("gu", "hT", "y")
        own = [(1, ("oT", 1)), (9, ("oT", 0))]
        maxima = spread(max0, 6, 8) + [(11, ("shift", 0))] + spread(max1, 12, 21) + [(23, ("shift", 1))]
        PLAN1 = slotted(spread([(k, f) for f in range(EG) for k in EXPERT], 1, 21), own, maxima)
        shared = spread([(k, f) for f in range(SG) for k in SHARED], 0, 20)
        PLAN2 = {
            NH: slotted(own, maxima, shared, [(10, ("rows", (0, 0))), (14, ("rows", (0, 1)))]),
            NH + 1: slotted(own, maxima, shared, spread([("add", (k, n)) for n in range(TC) for k in range(2)], 3, 22)),
            NH + 2: slotted(own, maxima, shared, spread([("add", (k, n)) for n in range(TC, NT) for k in range(2)], 3, 22)),
            NH + 3: slotted(own, shared, [(6, ("out", (TC, 0))), (10, ("out", (TC + 2, 0))), (12, ("rows", (1, 0))),
                                          (15, ("out", (0, 2))), (18, ("out", (2, 2)))]),
        }
        END = [("oT", 1), ("rows", (1, 1)), ("out", (TC, 1)), ("out", (TC + 2, 1))]
        PRE = max0 + [("shift", 0)] + max1 + [("shift", 1)]
        AB = 3

        def banked(plan):
            return [t for slot in plan for t in slot if t[0] != "add"]
        NPRE, N1 = len(PRE), len(banked(PLAN1))
        assert NPRE % AB == 0 and N1 % AB == 0
        before2, at = {}, NPRE + NH * N1
        for g in range(NH, NG):
            before2[g] = at
            at += len(banked(PLAN2[g]))
        before2[NG] = at

        def place(g, task, phase):
            if phase == 0:
                n = PRE.index(task)
                return 5 + n % AB, n + 1
            if phase == 1:
                n = banked(PLAN1).index(task)
                return 5 + n % AB, g * N1 + (NPRE + n + 1)
            n = before2[g] + (END if g == NG else banked(PLAN2[g])).index(task)
            return 5 + n % AB, n + 1

        def factor(n, m):
            return HD ** -0.5 if n == 0 else C1 if (n, m) == (2, 0) else 1.0

        SPLIT_ORDER = [(0, 0), (1, 0), (0, 1), (1, 1), (2, 1), (2, 0), (3, 1), (3, 0)]

        def shape_of(ic, jb):
            off = max(0, jb * P - ic * CH)
            return off, jb // TC == ic

        @block.gpsimd
        def _(pool):
            steps = [0]

            def link(ins):
                steps[0] += 1
                ins.then_inc(pool_step, 1)
                pool.wait_ge(pool_step, steps[0])

            def select(t, op, fill, base, pattern, mult):
                return nc.gpsimd.affine_select(out=t, in_=t, compare_op=op, fill=fill, base=base,
                                               pattern=pattern, channel_multiplier=mult)
            nc.gpsimd.memset(blockm[:, :, :], 1.0)
            nc.gpsimd.memset(zero_i[:, :], 0)
            link(nc.gpsimd.memset(ident[:, :], 0.0))
            select(ident[:, :], ALU.not_equal, 1.0, 0, [[-1, P]], 1).then_inc(ident_ready, 1)
            pool.wait_ge(ident_ready, 1)
            for half in range(2):
                rows = blockm[64 * half:64 * half + 64, :, :]
                link(select(rows, ALU.is_ge, 0.0, 0, [[-NS, 8], [0, HD]], 1))
                ins = select(rows, ALU.is_ge, 0.0, NS - 1, [[NS, 8], [0, HD]], -1)
                ins.then_inc(block_ready, 1)
                pool.wait_ge(block_ready, half + 1)
            pool.dma_start(ids_d[0:DUMP, :].rearrange("(e c) o -> e (c o)", c=CAP), zero_i[:, :]).then_inc(ids0_out, 16)
            nc.gpsimd.iota(iota_i[:, :, :], [[T, 2], [P, NT]], base=DUMP, channel_multiplier=1)
            nc.gpsimd.iota(tok[:, :], [[P, NT]], base=0, channel_multiplier=1)
            nc.gpsimd.iota(iota_r[:, :, :], [[0, NT], [-1, E]], base=E, channel_multiplier=0,
                           allow_small_or_imprecise_dtypes=True)
            link(nc.gpsimd.iota(iota_s[:, :, :], [[0, NT], [CAP, E]], base=0, channel_multiplier=0,
                                allow_small_or_imprecise_dtypes=True))
            nc.gpsimd.tensor_copy(dump[:, :, :], iota_i[:, :, :])
            nc.gpsimd.memset(ident_b[:, :], 0.0)
            nc.gpsimd.memset(mask_t[:, :], 0.0)
            nc.gpsimd.memset(mask_n[:, :], 0.0)
            nc.gpsimd.memset(upper[:, :], 1.0)
            link(nc.gpsimd.memset(ones_b[:, :], 1.0))
            select(ident_b[:, :], ALU.not_equal, 1.0, 0, [[-1, P]], 1)
            select(mask_t[:, :], ALU.is_ge, NEG, 0, [[1, P]], -1)
            select(mask_n[:, :], ALU.is_ge, NEG, 0, [[-1, P]], 1)
            link(select(upper[:, :], ALU.is_gt, 0.0, 0, [[1, P]], -1))
            for n in range(4):
                link(nc.gpsimd.memset(stage[n][KR:KS, :, :, :], float(n % 2)))
            nc.gpsimd.memset(v_st[:, :, :, :, HD:], 1.0).then_inc(consts, 1)

            for at in range(4):
                n, m = SPLIT_ORDER[at]
                pool.wait_ge(second_rest, at + 1)
                pool.wait_ge(second_part, at + 1)
                nc.gpsimd.tensor_tensor(split[:, n, 2, m, :], rest_[:, at % 2, :], split[:, n, 1, m, :],
                                        ALU.subtract).then_inc(parts_ready, 1)

            pool.wait_ge(ids0_out, 16)
            pool.wait_ge(slots_ready, 2)
            for k in range(2):
                for n in range(NT):
                    nc.gpsimd.indirect_dma_start(
                        out=ids_d[:, :], out_offset=bass.IndirectOffsetOnAxis(ap=sidx[:, k, n:n + 1], axis=0),
                        in_=tok[:, n:n + 1], in_offset=None).then_inc(ids_out, 16)
            pool.wait_ge(ids_out, 16 * 2 * NT)
            with nc.allow_non_contiguous_dma(reason="2,048 ids"):
                pool.dma_start(ids_sb[:, :], ids_d[0:DUMP, :].rearrange("(e c) o -> c (e o)", c=CAP)).then_inc(ids_in, 16)
            pool.wait_ge(ids_in, 16)
            pool.wait_ge(xn_out, 16)

            def values(g):
                src = v_all[:, :, bass.ds(g * (GH * HD), GH * HD)].rearrange("p n (h d) -> p n h d", h=GH)
                dst = v_st[:, bass.ds(g % 2, 1), :, :, 0:HD].rearrange("p o n h d -> p (o n) h d")
                nc.gpsimd.tensor_copy(dst, src).then_inc(v_ready, 1)

            def gather(g, f, first):
                if not first:
                    pool.wait_ge(aux_full, place(g - 1, ("xT", f), 1)[1])
                    pool.wait_ge(xe_in[f], 16 * g)
                nc.gpsimd.tensor_copy(ids_cur[:, f, :], ids_sb[:, bass.ds(g * EG + f, 1)]).then_inc(pool_ids, 1)
                pool.wait_ge(pool_ids, g * EG + (f + 1))
                pool.nop(nofuse=True)
                nc.gpsimd.indirect_dma_start(
                    out=xe[:, f, :], out_offset=None, in_=xn_d[:, :],
                    in_offset=bass.IndirectOffsetOnAxis(ap=ids_cur[:, f, :], axis=0)).then_inc(xe_in[f], 16)

            for f in range(EG):
                gather(0, f, True)
            pool.wait_ge(v_done, NT // 2)
            values(0)
            values(1)
            with pool.Fori(1, NH) as g:
                for f in range(EG):
                    gather(g, f, False)
                pool.wait_ge(acc_full, g * NC)
                values(g + 1)

            for f in range(EG):
                pool.wait_ge(ye_out[f], 16 * NH)
            for g in range(NH, NG - 1):
                for n in range({NH: NT}.get(g, 0)):
                    for k in range(2):
                        nc.gpsimd.indirect_dma_start(
                            out=gath[:, k, n, :], out_offset=None, in_=ye_d[:, :],
                            in_offset=bass.IndirectOffsetOnAxis(ap=gidx[:, k, n:n + 1], axis=0)).then_inc(gath_in[n], 16)
                    if n == 1:
                        pool.wait_ge(acc_full, g * NC)
                        values(g + 1)
                if g > NH:
                    pool.wait_ge(acc_full, g * NC)
                    values(g + 1)


        def shift_rows(queue, g, ic, pr, phase):
            queue.wait_ge(aux_free, place(g, ("shift", ic), phase)[1])
            for hl in range(2):
                for h in range(GH):
                    row = (hl * GH + h) * TC
                    queue.dma_start(qs[KR + hl:KR + hl + 1, pr, h, ic * CH:(ic + 1) * CH],
                                 mT[row:row + TC, ic, :]).then_inc(shift_in[ic], 16)

        @block.sync
        def _(sp):
            w_v = wqkvo.rearrange("w (k p) d -> p w k d", p=P)
            for n in range(NC):
                sp.dma_start(acc[:, n * TC:(n + 1) * TC, :],
                             x[n * CH:(n + 1) * CH, :].rearrange("(n p) d -> p n d", p=P)).then_inc(x_in[n], 16)
            for w in range(2):
                sp.dma_start(wt[:, w, :, :], w_v[:, w, :, :]).then_inc(wqk_in, 16)
            for w in range(2, 4):
                sp.dma_start(wt[:, w, :, :], w_v[:, w, :, :]).then_inc(wvo_in, 16)
            sp.wait_ge(xn_ready, NT)
            sp.dma_start(xn_d.rearrange("(n p) d -> p n d", p=P), xn[:, :, :]).then_inc(xn_out, 16)
            def parts_to_dram(at):
                n, m = SPLIT_ORDER[at]
                sp.wait_ge(parts_ready, at + 1)
                for s in range(SPL):
                    slot = s if n % 2 == 0 else SPL - 1 - s
                    if n < 2:
                        dst = parts_d[n][m * NS:(m + 1) * NS, slot, :, :]
                    else:
                        dst = parts_d[n][:, slot, m * NS:(m + 1) * NS, :]
                    sp.dma_start(dst, split[:, n, s, m, :]).then_inc(parts_out[at], 16)

            def load_rows(g, pr, n, done):
                for row, qp, num, kp in RUNS:
                    part = qp if n % 2 == 0 else kp
                    src = parts_d[n][bass.ds(g * GH, GH), part:part + num, :, :].rearrange("h s r t -> (s r) h t")
                    sp.dma_start(stage[n][row * HD:(row + num) * HD, pr, :, :], src).then_inc(done, 16)

            def load_qk(g, pr):
                load_rows(g, pr, 0, qk_in[pr])
                load_rows(g, pr, 1, qk_in[pr])

            def load_f(g, pr):
                load_rows(g, pr, 2, f_in[pr])
                load_rows(g, pr, 3, f_in[pr])
                load_gaps(g, pr)

            def load_gaps(g, pr):
                sp.dma_start(fq[KR:KS, pr, :, :], gap_d[bass.ds(g, 1), :, :, :].rearrange("o s h t -> (o s) h t")).then_inc(f_in[pr], 16)

            parts_to_dram(0)
            parts_to_dram(1)
            for at in range(2):
                sp.wait_ge(parts_out[at], 16 * SPL)
            sp.wait_ge(consts, 1)
            load_qk(0, 0)
            for f in range(EG):
                sp.dma_start(w13_sb[:, f, :, :], w13[f, :, :].rearrange("(k p) i -> p k i", p=P)).then_inc(w_in[f], 16)
                sp.dma_start(w2_sb[:, f, :, :], w2[f, :, :].rearrange("(k p) d -> p k d", p=I2)).then_inc(w_in[f], 16)
            sp.dma_start(gap_d.rearrange("g s h t -> s g (h t)"),
                         fq[KR:KS, 0:1, :, :].rearrange("s o h t -> s o (h t)").to_broadcast((2, NG, GH * T))).then_inc(zeros_out, 16)
            for at in range(2, 6):
                parts_to_dram(at)
            for at in range(2, 6):
                sp.wait_ge(parts_out[at], 16 * SPL)
            load_rows(0, 0, 2, f_in[0])
            for at in range(6, 8):
                parts_to_dram(at)
            for at in range(6, 8):
                sp.wait_ge(parts_out[at], 16 * SPL)
            sp.wait_ge(wide_ready, 1)
            sp.wait_ge(zeros_out, 16)
            needed = sp.value_load(wide[0:1, 0:1], min_val=0, max_val=1)
            with sp.If(needed > 0):
                with sp.Fori(0, NG) as g:
                    sp.wait_ge(own_turned, g + 1)
                    sp.nop(nofuse=True)
                    for n in range(4):
                        load_rows(g, 1, n, own_in)
                    sp.wait_ge(own_rows, g + 1)
                    sp.nop(nofuse=True)
                    sp.dma_start(gap_d[bass.ds(g, 1), :, :, :].rearrange("o s h (i t) -> (o s h i) t", t=P),
                                 own_T[:, :]).then_inc(own_out, 16)
                    sp.wait_ge(own_out, (g + 1) * 16)
                    sp.nop(nofuse=True)
            load_rows(0, 0, 3, f_in[0])
            load_gaps(0, 0)
            shift_rows(sp, -1, 1, 0, 0)

            def expert_out(g, f):
                sp.wait_ge(aux_free, place(g, ("y", f), 1)[1])
                sp.dma_start(ye_d[bass.ds((g * EG + f) * CAP, CAP), :], ye[:, f, :]).then_inc(ye_out[f], 16)

            def expert_in(g, f):
                sp.dma_start(w13_sb[:, f, :, :], w13[bass.ds(g * EG + f, 1), :, :]
                             .rearrange("o (k p) i -> p (o k) i", p=P)).then_inc(w_in[f], 16)
                sp.dma_start(w2_sb[:, f, :, :], w2[bass.ds(g * EG + f, 1), :, :]
                             .rearrange("o (k p) d -> p (o k) d", p=I2)).then_inc(w_in[f], 16)

            def body(g, pr, phase):
                if phase == 1 or g < NG - 1:
                    sp.wait_ge(acc_full, g * NC)
                    load_qk(g + 1, 1 - pr)
                    load_f(g + 1, 1 - pr)
                if phase == 1:
                    for f in range(EG):
                        if f == EG // 2:
                            shift_rows(sp, g, 0, 1 - pr, phase)
                        expert_out(g, f)
                        if isinstance(g, int) and g == NH - 1:
                            if f == 0:
                                sp.dma_start(w13_sb[:, 0, :, :], ws13.rearrange("(k p) i -> p k i", p=P)).then_inc(ws_in, 16)
                                sp.dma_start(w2_sb[:, 0, :, :], ws2.rearrange("(k p) d -> p k d", p=I2)).then_inc(ws_in, 16)
                        else:
                            expert_in(g + 1, f)
                if phase == 1 or g < NG - 1:
                    for ic in range(1 if phase == 1 else 0, NC):
                        shift_rows(sp, g, ic, 1 - pr, phase)

            with sp.Fori(0, NH // 2 - 1) as it:
                body(it * 2, 0, 1)
                body(it * 2 + 1, 1, 1)
            body(NH - 2, 0, 1)
            body(NH - 1, 1, 1)
            for g in range(NH, NG):
                body(g, g % 2, 2)
            for g, n in ((NG - 1, 0), (NG - 1, 2), (NG, TC), (NG, TC + 2)):
                sp.wait_ge(aux_free, place(g, ("out", (n, 2 if n < TC else 1)), 2)[1])
                sp.dma_start(out[n * P:(n + 2) * P, :].rearrange("(n p) d -> p n d", p=P), acc[:, n:n + 2, :]).then_inc(y_out, 16)
            sp.wait_ge(y_out, 16 * 4)

        @block.scalar
        def _(act):
            A = nc.scalar.activation
            for dst, src in ((pos[:, :], positions), (dire[:, :], directions), (LS, log_scales), (LA, log_amplitudes)):
                act.dma_start(dst, src).then_inc(par_in, 16)
            for dst, src in ((PS, sensitivity), (DS, strength), (GG, gsa_gate)):
                act.dma_start(dst, src.to_broadcast((P, 1))).then_inc(par_in, 16)
            act.dma_start(gw_sb[:, :, :], gate_w.rearrange("(k p) e -> p k e", p=P)).then_inc(gate_in, 16)
            act.dma_start(gb_sb[:, 0, :], gate_b.to_broadcast((P, E))).then_inc(gate_in, 16)
            act.wait_ge(var_ready, 1)
            A(vstd[:, 1, :], vstd[:, 0, :], ACT.Sqrt).then_inc(var_root, 1)
            act.wait_ge(norm_ready, 1)
            A(NRM, NSQ, ACT.Sqrt).then_inc(norm_root, 1)

            def bank_ready(n):
                act.wait_ge(pro_full, n + 1)
                return ps[:, n % PB, :]

            def evacuate(n):
                kind, a = PRO[n]
                b = bank_ready(n)
                if kind == "xnT":
                    k, tq = a
                    A(xnT[:, k, tq * CH:(tq + 1) * CH], b, ACT.Copy).then_inc(pro_act, 1)
                elif kind == "proj":
                    s, m, tc = a
                    A(qkT[:, s, m, tc * CH:(tc + 1) * CH], b, ACT.Copy).then_inc(pro_act, 1)
                elif kind == "feat":
                    s, tc, w = a
                    A(feat[:, s, w, tc * CH:(tc + 1) * CH], b, ACT.Exp if w == 0 else ACT.Tanh,
                      bias=BG if w == 0 else BD).then_inc(pro_act, 1)
                else:
                    A(v_all[:, 2 * a:2 * a + 2, :].rearrange("p n d -> p (n d)"), b, ACT.Copy).then_inc(v_done, 1)

            def part0(at):
                n, m = SPLIT_ORDER[at]
                src = qkT[:, n, m, :] if n < 2 else feat[:, n - 2, m, :]
                if n < 2:
                    act.wait_ge(pro_act, reads[PRO.index(("proj", (n, m, 1)))][1])
                else:
                    act.wait_ge(features, n - 1)
                A(split[:, n, 0, m, :], src, ACT.Copy, scale=factor(n, m)).then_inc(first_part, 1)

            def part1(at):
                n, m = SPLIT_ORDER[at]
                act.wait_ge(second_rest, at + 1)
                A(split[:, n, 1, m, :], rest_[:, at % 2, :], ACT.Copy).then_inc(second_part, 1)

            def square(s, m):
                act.wait_ge(pro_act, reads[PRO.index(("proj", (s, m, 1)))][1])
                A(sq[s][:, m, :], qkT[:, s, m, :], ACT.Square).then_inc(squares, 1)

            tasks = [n for n, (k, _) in enumerate(PRO) if READER[k] == "act"]
            act.wait_ge(par_in, 16 * 7)
            A(IS2, LS, ACT.Exp, scale=-2.0)
            A(AMP, LA, ACT.Exp)
            A(EG_, GG, ACT.Exp, scale=-1.0).then_inc(par_exp, 1)
            for n in tasks[:6]:
                evacuate(n)
            part0(0)
            act.wait_ge(gate_dve, 1)
            A(g_[2][:, :, :], g_[1][:, :, :], ACT.Exp, scale=-1.0).then_inc(gate_act, 1)
            evacuate(tasks[6])
            act.wait_ge(gate_dve, 2)
            A(g_[4][:, :, :], g_[3][:, :, :], ACT.Ln).then_inc(gate_act, 1)
            evacuate(tasks[7])
            part0(1)
            act.wait_ge(gate_dve, 3)
            A(g_[10][:, :, :], g_[11][:, :, :], ACT.Sqrt).then_inc(gate_act, 1)
            part1(0)
            evacuate(tasks[8])
            evacuate(tasks[9])
            square(0, 0)
            square(0, 1)
            part1(1)
            evacuate(tasks[10])
            evacuate(tasks[11])
            square(1, 0)
            square(1, 1)
            part0(2)
            part0(3)
            act.wait_ge(gw_ready, 1)
            for n in tasks[12:16]:
                evacuate(n)
            part1(2)
            part1(3)
            for n in tasks[16:20]:
                evacuate(n)
            part0(4)
            part0(5)
            part1(4)
            part1(5)
            part0(6)
            part0(7)
            for n in tasks[20:]:
                evacuate(n)
            part1(6)
            part1(7)

            shift_rows(act, -1, 0, 0, 0)
            act.wait_ge(parts_ready, 8)

            def body(g, plan, phase):
                for p, (ic, jb) in enumerate(PAIRS):
                    for turn in range(4):
                        var, s = divmod(turn, 2)
                        ready, done = (std_ready, std_exp) if var == 0 else (gsa_ready, gsa_exp)
                        off, _ = shape_of(ic, jb + s)
                        act.wait_ge(ready, g * (2 * NP) + (2 * p + s + 1))
                        A(probs[:, var, s, :, off:CH], ps[:, 1 + 2 * s:3 + 2 * s, off:CH], ACT.Exp).then_inc(done, 1)
                        for t in plan[4 * p + turn]:
                            if t[0] == "gu":
                                bank, count = place(g, t, phase)
                                act.wait_ge(aux_full, count)
                                A(th[:, :], ps[:, bank, 0:I], ACT.Tanh, scale=0.5).then_inc(th_ready, 1)

            with act.Fori(0, NH) as g:
                body(g, PLAN1, 1)
            for g in range(NH, NG):
                body(g, PLAN2[g], 2)

        @block.tensor
        def _(pe):
            M = nc.tensor.matmul
            pe.wait_ge(ident_ready, 1)

            def take(n):
                if n >= PB:
                    s, c = reads[n - PB]
                    if PRO[n - PB][0] == "v":
                        s = v_done
                    pe.wait_ge(s, c)
                return ps[:, n % PB, :]

            for n, (kind, a) in enumerate(PRO):
                b = take(n)
                if kind == "xnT":
                    k, tq = a
                    for i in range(TC):
                        t = tq * TC + i
                        pe.wait_ge(xn_ready, t + 1)
                        last = nc.tensor.transpose(b[:, i * P:(i + 1) * P], xn[:, t, k * P:(k + 1) * P], ident[:, :])
                elif kind == "par":
                    pe.wait_ge(gw_ready, 1)
                    for w in range(3):
                        nc.tensor.transpose(b[:, w * P:(w + 1) * P], gwide[:, w, :], ident[:, :])
                    last = nc.tensor.transpose(b[0:1, 3 * P:4 * P], BND, ident[:, :])
                elif kind == "gate":
                    pe.wait_ge(gate_in, 32)
                    pe.wait_ge(pro_act, KD * NC)
                    for t in range(NT):
                        for k in range(KD):
                            last = M(b[:, t * E:(t + 1) * E], xnT[:, k, t * P:(t + 1) * P], gw_sb[:, k, :],
                                     start=k == 0, stop=k == KD - 1)
                elif kind == "proj":
                    s, m, tc = a
                    pe.wait_ge(wqk_in, 32)
                    pe.wait_ge(pro_act, KD * (tc + 1))
                    for k in range(KD):
                        last = M(b, wt[:, s, k, m * P:(m + 1) * P], xnT[:, k, tc * CH:(tc + 1) * CH],
                                 start=k == 0, stop=k == KD - 1)
                elif kind == "feat":
                    s, tc, w = a
                    pe.wait_ge(pro_dve, 2)
                    pe.wait_ge(squares, 2 * s + 2)
                    for m in range(KD):
                        half = slice(64 * m, 64 * m + 64)
                        cols = slice(tc * CH, (tc + 1) * CH)
                        if w == 0:
                            M(b[half, :], gT[:, 0, half], sq[s][:, m, cols], start=True, stop=False)
                            last = M(b[half, :], gT[:, 1, half], qkT[:, s, m, cols], start=False, stop=True)
                        else:
                            last = M(b[half, :], gT[:, 2, half], qkT[:, s, m, cols], start=True, stop=True)
                elif kind == "cum":
                    pe.wait_ge(ohs_ready, 1)
                    pe.wait_ge(consts, 1)
                    M(b[:, 0:NT * E], upper[:, :], ohs[:, :, :].rearrange("p n e -> p (n e)"), start=True, stop=False)
                    for t in range(NT - 1):
                        rest = NT - 1 - t
                        last = M(b[:, (t + 1) * E:NT * E].rearrange("p (n e) -> p n e", e=E), ones_b[:, :],
                                 ohs[:, t:t + 1, :].to_broadcast((P, rest, E)), start=False, stop=t == NT - 2)
                else:
                    pe.wait_ge(wvo_in, 32)
                    for i in range(2):
                        for k in range(KD):
                            last = M(b[:, i * D:(i + 1) * D], xnT[:, k, (2 * a + i) * P:(2 * a + i + 1) * P],
                                     wt[:, 2, k, :], start=k == 0, stop=k == KD - 1)
                last.then_inc(pro_full, 1)

            def aux(g, t, phase, pr):
                kind, a = t
                if kind == "add":
                    return
                bank, count = place(g, t, phase)
                b = ps[:, bank, :]
                if not isinstance(count, int) or count > AB:
                    pe.wait_ge(aux_free, count - AB)
                if kind == "max2":
                    for it in range(2):
                        n0, n1 = it * P, it * 2 * P + P
                        M(b[:, n0:n1], qs[0:KR, pr, a[0], it * P:(it + 1) * P], ks[0:KR, pr, a[0], 0:(it + 1) * P],
                          start=True, stop=False)
                        ins = M(b[:, n1 - P:n1], ident_b[:, :], mask_n[:, :], start=False, stop=True)
                elif kind == "max":
                    h, it, pc = a
                    n0, n1 = pc * CH, min((it + 1) * P, (pc + 1) * CH)
                    diag = n1 == (it + 1) * P
                    lhs = qs[0:KR, pr, h, it * P:(it + 1) * P]
                    ins = M(b[:, 0:n1 - n0], lhs, ks[0:KR, pr, h, n0:n1], start=True, stop=not diag)
                    if diag:
                        ins = M(b[:, n1 - n0 - P:n1 - n0], ident_b[:, :], mask_n[:, :], start=False, stop=True)
                elif kind == "shift":
                    pe.wait_ge(mhl_ready, (g + 1) * NC + (a + 1))
                    ins = nc.tensor.transpose(psb[0:2 * GH * TC, bank, 0:P],
                                              mhl[:, a, :, :].rearrange("p s c -> p (s c)"), ident_b[:, :])
                elif kind == "xT":
                    pe.wait_ge(xe_in[a], (g + 1) * 16)
                    for k in range(KD):
                        ins = nc.tensor.transpose(b[:, k * P:(k + 1) * P], xe[:, a, k * P:(k + 1) * P], ident[:, :])
                elif kind == "gu":
                    if phase == 1:
                        pe.wait_ge(aux_free, place(g, ("xT", a), phase)[1])
                        pe.wait_ge(w_in[a], (g + 1) * 32)
                    else:
                        pe.wait_ge(ws_in, 32)
                    t0 = (g - NH) * SG + a if phase == 2 else 0
                    for k in range(KD):
                        lhs = xeT[:, k, :] if phase == 1 else xnT[:, k, t0 * P:(t0 + 1) * P]
                        ins = M(b[:, 0:2 * I], lhs, w13_sb[:, a if phase == 1 else 0, k, :], start=k == 0, stop=k == KD - 1)
                elif kind == "hT":
                    pe.wait_ge(aux_free, place(g, ("gu", a), phase)[1])
                    for c in range(2):
                        ins = nc.tensor.transpose(b[0:I2, c * P:(c + 1) * P], hh[:, c * I2:(c + 1) * I2], ident[:, :])
                elif kind == "y":
                    pe.wait_ge(aux_free, place(g, ("hT", a), phase)[1])
                    for c in range(2):
                        ins = M(b[:, 0:D], hT[:, c, :], w2_sb[:, a if phase == 1 else 0, c, :], start=c == 0, stop=c == 1)
                elif kind == "oT":
                    pe.wait_ge(acc_free, g * NC + (2 if a == 1 else 3))
                    for i in range(TC):
                        ins = nc.tensor.transpose(b[:, i * P:(i + 1) * P], pv_sb[:, i * P:(i + 1) * P], ident[:, :])
                elif kind == "rows":
                    k, tq = a
                    pe.wait_ge(o_ready, NH * NC + 1 if k == 0 else NG * NC + tq)
                    for i in range(TC):
                        ins = nc.tensor.transpose(b[:, i * P:(i + 1) * P], o_nat[:, tq * TC + i, GW + k * P:GW + (k + 1) * P], ident[:, :])
                else:
                    n, k = a
                    for rows in (("rows", (0, 0)), ("rows", (0, 1))) if k == 0 else (("rows", (1, 0 if n < TC else 1)),):
                        at = NH if k == 0 else NG - 1 if n < TC else NG
                        pe.wait_ge(aux_free, place(at, rows, 2)[1])
                    if k:
                        pe.wait_ge(aux_free, place(NH, ("rows", (0, 1)), 2)[1])
                    ks_ = (0, 1) if k == 2 else (k,)
                    for i in range(2):
                        for kk in ks_:
                            ins = M(b[:, i * D:(i + 1) * D], oT[:, kk, (n + i) * P:(n + i + 1) * P], wt[:, 3, kk, :],
                                    start=kk == ks_[0], stop=kk == ks_[-1])
                ins.then_inc(aux_full, 1)

            pe.wait_ge(wide_ready, 1)
            pe.wait_ge(pro_act, reads[len(PRO) - NT // 2 - 1][1])
            pe.wait_ge(v_done, NT // 2)
            pe.wait_ge(consts, 1)
            needed = pe.value_load(wide[0:1, 0:1], min_val=0, max_val=1)
            with pe.If(needed > 0):
                with pe.Fori(0, NG) as g:
                    pe.wait_ge(own_in, (g + 1) * (16 * 12))
                    for n in range(GH * NT):
                        h, it = divmod(n, NT)
                        cols = [(pc, pc * CH, min((it + 1) * P, (pc + 1) * CH)) for pc in range(it // TC + 1)]
                        pe.wait_ge(own_read, g * (GH * NT) + (n + 1))
                        for pc, n0, n1 in cols:
                            diag = n1 == (it + 1) * P
                            ins = M(ps[:, 1 + pc, 0:n1 - n0], qs[0:KR, 1, h, it * P:(it + 1) * P], ks[0:KR, 1, h, n0:n1],
                                    start=True, stop=not diag)
                            if diag:
                                ins = M(ps[:, 1 + pc, n1 - n0 - P:n1 - n0], ident_b[:, :], mask_n[:, :], start=False, stop=True)
                        ins.then_inc(own_plain, 1)
                        pe.wait_ge(own_plain_read, g * (GH * NT) + (n + 1))
                        for pc, n0, n1 in cols:
                            ins = M(ps[:, 1 + pc, 0:n1 - n0], fq[0:KR, 1, h, it * P:(it + 1) * P], fk[0:KR, 1, h, n0:n1],
                                    start=False, stop=True, skip_group_check=True)
                        ins.then_inc(own_full, 1)
                    pe.wait_ge(own_split, g + 1)
                    nc.tensor.transpose(psb[0:2 * GH * NT, 3, 0:P], own_hl[:, :, :, :].rearrange("p s h n -> p (s h n)"),
                                        ident_b[:, :]).then_inc(own_turned, 1)

            pe.wait_ge(qk_in[0], 96)
            def std(g, pr, p, s):
                ic, jb = PAIRS[p]
                off, diag = shape_of(ic, jb + s)
                if s == 0 and jb == 0:
                    pe.wait_ge(shift_in[ic], (g + 1) * 64)
                before = g * (2 * NP) + (2 * (p - 1) + s + 1)
                if not isinstance(before, int) or before > 0:
                    pe.wait_ge(gsa_exp, before)
                for h in range(GH):
                    b = ps[:, 1 + 2 * s + h, :]
                    ins = M(b[:, off:CH], ks[:, pr, h, (jb + s) * P:(jb + s + 1) * P],
                            qs[:, pr, h, ic * CH + off:(ic + 1) * CH], start=True, stop=not diag)
                    if diag:
                        ins = M(b[:, off:off + P], ident_b[:, :], mask_t[:, :], start=False, stop=True)
                ins.then_inc(std_ready, 1)

            def splat(g, pr, p, s):
                ic, jb = PAIRS[p]
                off, _ = shape_of(ic, jb + s)
                pe.wait_ge(std_exp, g * (2 * NP) + (2 * p + s + 1))
                for h in range(GH):
                    ins = M(ps[:, 1 + 2 * s + h, off:CH], fk[:, pr, h, (jb + s) * P:(jb + s + 1) * P],
                            fq[:, pr, h, ic * CH + off:(ic + 1) * CH], start=False, stop=True,
                            skip_group_check=True)
                ins.then_inc(gsa_ready, 1)

            def pv(g, pr, p, s):
                ic, jb = PAIRS[p]
                off, _ = shape_of(ic, jb + s)
                if jb + s == 0:
                    pe.wait_ge(acc_free, g * NC + (ic + 2))
                    pe.wait_ge(v_ready, g + 1)
                pe.wait_ge(gsa_exp, g * (2 * NP) + (2 * p + s + 1))
                end = jb + s == (ic + 1) * TC - 1
                for var in range(2):
                    for h in range(GH):
                        c = 2 * HD * (var * GH + h)
                        ins = M(ps[c:c + 2 * HD, 0, off:CH], v_st[:, pr, jb + s, h, :],
                                probs[:, var, s, h, off:CH], start=jb + s == 0, stop=end)
                if end:
                    ins.then_inc(acc_full, 1)

            def body(g, pr, plan, phase, half):
                nxt = half + pr
                last = phase == 2 and g == NG - 1

                def slot(n):
                    for t in plan[n]:
                        if t[0] in ("max", "max2"):
                            pe.wait_ge(qk_in[1 - pr], (nxt + 1) * 96)
                        aux(g, t, phase, 1 - pr)

                pe.wait_ge(f_in[pr], (half + 1) * 112)
                for p in range(NP):
                    slot(4 * p)
                    splat(g, pr, p, 0)
                    slot(4 * p + 1)
                    splat(g, pr, p, 1)
                    slot(4 * p + 2)
                    for s in range(2):
                        pv(g, pr, p, s)
                        if p + 1 < NP:
                            std(g, pr, p + 1, s)
                        elif not last:
                            if s == 0:
                                pe.wait_ge(qk_in[1 - pr], (nxt + 1) * 96)
                            std(g + 1, 1 - pr, 0, s)
                        if s == 0:
                            slot(4 * p + 3)

            for t in PRE:
                if t == ("shift", 1):
                    std(0, 0, 0, 0)
                    std(0, 0, 0, 1)
                aux(-1, t, 0, 0)
            with pe.Fori(0, NH // 2) as it:
                body(it * 2, 0, PLAN1, 1, it)
                body(it * 2 + 1, 1, PLAN1, 1, it)
            for g in range(NH, NG):
                body(g, g % 2, PLAN2[g], 2, g // 2)
            for t in END:
                aux(NG, t, 2, 0)

        @block.vector
        def _(dve):
            V = nc.vector
            steps, base = [0], [0]

            def link(ins):
                steps[0] += 1
                ins.then_inc(dve_step, 1)
                dve.wait_ge(dve_step, base[0] + steps[0])

            def tt(out, a, b, op):
                return V.tensor_tensor(out, a, b, op)

            def rest_of(at):
                n, m = SPLIT_ORDER[at]
                src = qkT[:, n, m, :] if n < 2 else feat[:, n - 2, m, :]
                dve.wait_ge(first_part, at + 1)
                if at >= 2:
                    dve.wait_ge(parts_ready, at - 1)
                V.scalar_tensor_tensor(out=rest_[:, at % 2, :], in0=src, scalar=factor(n, m),
                                       in1=split[:, n, 0, m, :], op0=ALU.mult, op1=ALU.subtract).then_inc(second_rest, 1)

            def third_of(at):
                n, m = SPLIT_ORDER[at]
                dve.wait_ge(second_rest, at + 1)
                dve.wait_ge(second_part, at + 1)
                tt(split[:, n, 2, m, :], rest_[:, at % 2, :], split[:, n, 1, m, :], ALU.subtract).then_inc(parts_ready, 1)

            for t in range(NT):
                dve.wait_ge(x_in[t // TC], 16)
                ins = V.bn_stats(stats[:, t, :], acc[:, t, :])
            link(ins)
            for t in range(NT):
                ins = V.bn_aggr(mv[:, t, :], stats[:, t, :])
            link(ins)
            V.tensor_scalar(vstd[:, 0, :], mv[:, :, 1], EPS, None, ALU.add).then_inc(var_ready, 1)
            dve.wait_ge(var_root, 1)
            link(V.reciprocal(vstd[:, 0, :], vstd[:, 1, :]))
            for t in range(NT):
                V.tensor_scalar(xn[:, t, :], acc[:, t, :], mv[:, t, 0:1], vstd[:, 0, t:t + 1],
                                ALU.subtract, ALU.mult).then_inc(xn_ready, 1)
            dve.wait_ge(par_in, 16 * 7)
            tt(tmp16[:, 0, :], dire[:, :], dire[:, :], ALU.mult)
            link(tt(tmp16[:, 1, :], pos[:, :], pos[:, :], ALU.mult))
            V.reduce_sum(PP, tmp16[:, 1, :], AX.X)
            V.reduce_sum(NSQ, tmp16[:, 0, :], AX.X).then_inc(norm_ready, 1)
            dve.wait_ge(norm_root, 1)
            dve.wait_ge(par_exp, 1)
            dve.wait_ge(block_ready, 2)
            link(V.tensor_scalar(TMP, NRM, 1e-8, None, ALU.add))
            link(V.reciprocal(RN, TMP))
            V.tensor_scalar(HI2, IS2, -0.5, None, ALU.mult)
            V.tensor_scalar(tmp16[:, 3, :], pos[:, :], IS2, None, ALU.mult)
            V.tensor_scalar(C1, AMP, PS, None, ALU.mult)
            V.tensor_scalar(B1_, EG_, 1.0, None, ALU.add)
            link(V.tensor_scalar(tmp16[:, 2, :], dire[:, :], RN, None, ALU.mult))
            V.tensor_scalar(C2, C1, DS, None, ALU.mult)
            V.scalar_tensor_tensor(out=AD, in0=DS, scalar=-1.0, in1=DS, op0=ALU.mult, op1=ALU.max)
            V.scalar_tensor_tensor(out=AC, in0=C1, scalar=-1.0, in1=C1, op0=ALU.mult, op1=ALU.max)
            V.tensor_scalar(BG, HI2, PP, None, ALU.mult)
            V.reciprocal(B_, B1_)
            V.tensor_scalar(gwide[:, 0, :], blockm[:, :, :].rearrange("p h d -> p (h d)"), HI2, None, ALU.mult)
            tt(gwide[:, 1, :].rearrange("p (h d) -> p h d", d=HD), blockm[:, :, :],
               tmp16[:, 3:4, :].to_broadcast((P, NS, HD)), ALU.mult)
            tt(gwide[:, 2, :].rearrange("p (h d) -> p h d", d=HD), blockm[:, :, :],
               tmp16[:, 2:3, :].to_broadcast((P, NS, HD)), ALU.mult)
            link(tt(tmp16[:, 0, :], pos[:, :], tmp16[:, 2, :], ALU.mult))
            V.tensor_scalar(blendw[:, 2:3], B_, 0.15, 0.03, ALU.mult, ALU.min)
            V.scalar_tensor_tensor(out=BND, in0=AD, scalar=1.0, in1=AC, op0=ALU.add, op1=ALU.mult)
            link(V.reduce_sum(PD, tmp16[:, 0, :], AX.X))
            V.tensor_scalar(blendw[:, 3:4], blendw[:, 2:3], 1.0, None, ALU.mult)
            V.tensor_scalar(blendw[:, 0:1], blendw[:, 2:3], -1.0, 1.0, ALU.mult, ALU.add)
            V.tensor_scalar(blendw[:, 1:2], blendw[:, 2:3], -1.0, 1.0, ALU.mult, ALU.add)
            V.tensor_scalar(BD, PD, -1.0, None, ALU.mult).then_inc(gw_ready, 1)
            n = PRO.index(("gate", 0))
            flat = ps[:, n % PB, 0:NT * E].rearrange("p (n e) -> p n e", e=E)
            G = [g[:, :, :] for g in g_]
            R = [r_[:, n, :] for n in range(16)]

            def row(r):
                return r.unsqueeze(2).to_broadcast((P, NT, E))
            rest_of(0)
            dve.wait_ge(pro_full, n + 1)
            V.tensor_copy(G[0], flat).then_inc(pro_dve, 1)
            dve.wait_ge(pro_dve, 1)
            V.scalar_tensor_tensor(out=G[1], in0=G[0], scalar=-1.0, in1=G[0], op0=ALU.mult, op1=ALU.max).then_inc(gate_dve, 1)
            V.tensor_scalar(G[5], G[0], 0.0, None, ALU.max)
            dve.wait_ge(gate_act, 1)
            V.tensor_scalar(G[3], G[2], 1.0, None, ALU.add).then_inc(gate_dve, 1)
            dve.wait_ge(gate_dve, 2)
            link(V.tensor_scalar(G[6], G[3], -1.0, None, ALU.add))
            link(V.tensor_scalar(G[7], G[6], 0.0, None, ALU.is_equal))
            link(tt(G[6], G[6], G[7], ALU.add))
            V.reciprocal(G[8], G[6])
            link(tt(G[9], G[7], G[2], ALU.mult))
            link(tt(G[8], G[8], G[2], ALU.mult))
            dve.wait_ge(gate_act, 2)
            link(tt(G[8], G[8], G[4], ALU.mult))
            link(tt(G[8], G[8], G[9], ALU.add))
            tt(G[11], G[8], G[5], ALU.add).then_inc(gate_dve, 1)
            rest_of(1)
            dve.wait_ge(pro_full, PRO.index(("par", 0)) + 1)
            V.reduce_sum(bound[:, 0:H], ps[0:1, PRO.index(("par", 0)) % PB, 3 * P:4 * P].rearrange("p (h n) -> p h n", n=NS), AX.X)
            V.tensor_copy(gT[:, :, :].rearrange("p w c -> p (w c)"), ps[:, PRO.index(("par", 0)) % PB, 0:3 * P]).then_inc(pro_dve, 1)
            dve.wait_ge(gate_act, 3)
            link(tt(G[11], G[10], gb_sb[:, :, :].to_broadcast((P, NT, E)), ALU.add))
            choose, score, oh = G[11], G[10], [G[2], G[5]]
            dve.wait_ge(consts, 1)
            for k in range(2):
                link(V.reduce_max(R[0], choose, AX.X))
                link(tt(G[1], choose, row(R[0]), ALU.is_ge))
                link(tt(G[1], G[1], iota_r[:, :, :], ALU.mult))
                link(V.reduce_max(R[1], G[1], AX.X))
                link(tt(oh[k], G[1], row(R[1]), ALU.is_equal))
                if k == 0:
                    V.reduce_max(bound[:, H:H + 1], bound[:, 0:H], AX.X)
                    link(V.scalar_tensor_tensor(out=choose, in0=oh[0], scalar=NEG, in1=choose, op0=ALU.mult, op1=ALU.add))
                link(tt(G[1], oh[k], score, ALU.mult))
                link(V.reduce_sum(R[2 + k], G[1], AX.X))
            V.tensor_scalar(wide[:, :], bound[:, H:H + 1], SAFE, None, ALU.is_gt).then_inc(wide_ready, 1)
            tt(ohs[:, :, :], oh[0], oh[1], ALU.add).then_inc(ohs_ready, 1)
            link(tt(R[4], R[2], R[3], ALU.add))
            link(V.reciprocal(R[5], R[4]))

            def slots():
                n = PRO.index(("cum", 0))
                dve.wait_ge(pro_full, n + 1)
                V.tensor_copy(G[7], ps[:, n % PB, 0:NT * E].rearrange("p (n e) -> p n e", e=E)).then_inc(pro_dve, 1)
                dve.wait_ge(pro_dve, 3)
                link(tt(G[8], G[7], iota_s[:, :, :], ALU.add))
                for k in range(2):
                    tt(G[9], oh[k], G[7], ALU.mult)
                    link(tt(G[1], oh[k], G[8], ALU.mult))
                    V.reduce_sum(R[6], G[9], AX.X)
                    link(V.reduce_sum(R[7], G[1], AX.X))
                    link(V.tensor_scalar(R[8], R[6], float(CAP), None, ALU.is_lt))
                    tt(R[9], R[2 + k], R[5], ALU.mult)
                    tt(R[10], R[7], R[8], ALU.mult)
                    link(tt(R[11], R[7], dump[:, k, :], ALU.subtract))
                    tt(pairw[:, k, :], R[9], R[8], ALU.mult)
                    V.tensor_copy(gidx[:, k, :], R[10])
                    link(tt(R[12], R[11], R[8], ALU.mult))
                    link(tt(R[13], R[12], dump[:, k, :], ALU.add))
                    V.tensor_copy(sidx[:, k, :], R[13]).then_inc(slots_ready, 1)

            rest_of(2)
            rest_of(3)
            slots()
            for s in range(2):
                dve.wait_ge(pro_act, reads[PRO.index(("feat", (s, 1, 1)))][1])
                gs, dr = feat[:, s, 0, :], feat[:, s, 1, :]
                if s == 0:
                    V.scalar_tensor_tensor(out=dr, in0=gs, scalar=C2, in1=dr, op0=ALU.mult, op1=ALU.mult).then_inc(features, 1)
                else:
                    tt(dr, gs, dr, ALU.mult).then_inc(features, 1)
                rest_of(4 + 2 * s)
                rest_of(5 + 2 * s)
                third_of(4 + 2 * s)
                third_of(5 + 2 * s)
            dve.wait_ge(wide_ready, 1)
            needed = dve.value_load(wide[0:1, 0:1], min_val=0, max_val=1)
            with dve.If(needed > 0):
                V.memset(own_mx[:, :, :, :], 0.0).then_inc(own_read, 1)
                dve.wait_ge(own_read, 1)
                V.memset(own_hl[:, :, :, :], 0.0).then_inc(own_turned, 1)
                dve.wait_ge(own_turned, 1)
                both = ps[:, 1:3, :].rearrange("p b n -> p (b n)")
                with dve.Fori(0, NG) as g:
                    for n in range(GH * NT):
                        h, it = divmod(n, NT)
                        dve.wait_ge(own_plain, g * (GH * NT) + (n + 1))
                        V.reduce_max(own_mx[:, 0, h, it:it + 1], both[:, 0:(it + 1) * P], AX.X).then_inc(own_plain_read, 1)
                        dve.wait_ge(own_full, g * (GH * NT) + (n + 1))
                        V.reduce_max(own_mx[:, 1, h, it:it + 1], both[:, 0:(it + 1) * P], AX.X).then_inc(own_read, 1)
                    dve.wait_ge(own_plain_read, g * (GH * NT) + GH * NT)
                    dve.wait_ge(own_read, g * (GH * NT) + (GH * NT + 1))
                    tt(own_mx[:, 2, :, :], own_mx[:, 0, :, :], own_mx[:, 1, :, :], ALU.subtract).then_inc(own_step, 1)
                    dve.wait_ge(own_step, g * 2 + 1)
                    V.tensor_copy(own_hl[:, 0, :, :], own_mx[:, 2, :, :]).then_inc(own_step, 1)
                    dve.wait_ge(own_step, g * 2 + 2)
                    tt(own_hl[:, 1, :, :], own_mx[:, 2, :, :], own_hl[:, 0, :, :], ALU.subtract).then_inc(own_split, 1)
                    dve.wait_ge(own_turned, g + 2)
                    V.tensor_copy(own_T[:, :], psb[0:2 * GH * NT, 3, 0:P]).then_inc(own_rows, 1)
            V.memset(mx[:, :, :, :, :], 0.0).then_inc(acc_free, 1)
            dve.wait_ge(acc_free, 1)

            def aux(g, t, phase):
                kind, a = t
                if kind == "add":
                    k, n = a
                    dve.wait_ge(gath_in[n], 32)
                    link(V.scalar_tensor_tensor(out=acc[:, n, :], in0=gath[:, k, n, :], scalar=pairw[:, k, n:n + 1],
                                                in1=acc[:, n, :], op0=ALU.mult, op1=ALU.add))
                    return
                bank, count = place(g, t, phase)
                b = ps[:, bank, :]
                dve.wait_ge(aux_full, count)
                if kind == "max2":
                    V.reduce_max(mx[:, 0, a[0], 0, 0:1], b[:, 0:P], AX.X)
                    V.reduce_max(mx[:, 0, a[0], 1, 0:1], b[:, P:3 * P], AX.X).then_inc(aux_free, 1)
                elif kind == "max":
                    h, it, pc = a
                    n0, n1 = pc * CH, min((it + 1) * P, (pc + 1) * CH)
                    V.reduce_max(mx[:, it // TC, h, it % TC, pc:pc + 1], b[:, 0:n1 - n0], AX.X).then_inc(aux_free, 1)
                    if t == max0[-1] or t == max1[-1]:
                        ic = it // TC
                        dve.wait_ge(aux_free, count)
                        if ic == 0:
                            link(V.tensor_scalar(mneg[:, 0, :, :], mx[:, 0, :, :, 0], -1.0, None, ALU.mult))
                        else:
                            link(tt(mneg[:, 1, :, :], mx[:, 1, :, :, 0], mx[:, 1, :, :, 1], ALU.max))
                            link(V.tensor_scalar(mneg[:, 0, :, :], mneg[:, 1, :, :], -1.0, None, ALU.mult))
                        m32 = mneg[:, 0, :, :].rearrange("p h n -> p (h n)")
                        link(V.tensor_copy(mhl[:, ic, 0, :], m32))
                        tt(mhl[:, ic, 1, :], m32, mhl[:, ic, 0, :], ALU.subtract).then_inc(mhl_ready, 1)
                elif kind == "shift":
                    if phase:
                        dve.wait_ge(shift_in[a], (g + 1) * 64)
                    V.tensor_copy(mT[:, a, :], psb[0:2 * GH * TC, bank, 0:P]).then_inc(aux_free, 1)
                elif kind == "xT":
                    V.tensor_copy(xeT[:, :, :].rearrange("p k c -> p (k c)"), b[:, 0:D]).then_inc(aux_free, 1)
                elif kind == "gu":
                    first = g * EG + (a + 1) if phase == 1 else NH * EG + (g - NH) * SG + a + 1
                    dve.wait_ge(th_ready, first)
                    link(V.scalar_tensor_tensor(out=h1[:, :], in0=th[:, :], scalar=1.0, in1=b[:, 0:I], op0=ALU.add, op1=ALU.mult))
                    V.scalar_tensor_tensor(out=hh[:, :], in0=h1[:, :], scalar=0.5, in1=b[:, I:2 * I],
                                           op0=ALU.mult, op1=ALU.mult).then_inc(aux_free, 1)
                elif kind == "hT":
                    V.tensor_copy(hT[:, :, :].rearrange("p k c -> p (k c)"), b[0:I2, 0:2 * P]).then_inc(aux_free, 1)
                elif kind == "y":
                    if phase == 1:
                        dve.wait_ge(ye_out[a], g * 16)
                        V.tensor_copy(ye[:, a, :], b[:, 0:D]).then_inc(aux_free, 1)
                    else:
                        dst = acc[:, (g - NH) * SG + a, :]
                        tt(dst, b[:, 0:D], dst, ALU.add).then_inc(aux_free, 1)
                        dve.wait_ge(aux_free, count)
                elif kind == "oT":
                    o4 = b[:, :].rearrange("p (n v c) -> p n v c", n=TC, v=4)
                    link(V.reciprocal(rec[:, :, :], o4[:, :, :, HD]))
                    link(tt(recw[:, :, :], rec[:, :, :], blendw[:, :].unsqueeze(1).to_broadcast((P, TC, 4)), ALU.mult))
                    tt(onv[:, :, :, :], o4[:, :, :, 0:HD], recw[:, :, :].unsqueeze(3).to_broadcast((P, TC, 4, HD)), ALU.mult).then_inc(aux_free, 1)
                    dve.wait_ge(aux_free, count)
                    col = g * GW if a == 1 else g * GW + GW
                    dst = o_nat[:, a * TC:(a + 1) * TC, bass.ds(col, GW)].rearrange("p n (h d) -> p n h d", h=GH)
                    tt(dst, onv[:, :, 0:2, :], onv[:, :, 2:4, :], ALU.add).then_inc(o_ready, 1)
                elif kind == "rows":
                    k, tq = a
                    V.tensor_copy(oT[:, k, tq * CH:(tq + 1) * CH], b).then_inc(aux_free, 1)
                else:
                    n, k = a
                    dst = acc[:, n:n + 2, :].rearrange("p n d -> p (n d)")
                    tt(dst, b, dst, ALU.add).then_inc(aux_free, 1)
                    dve.wait_ge(aux_free, count)

            def evac(g, ic):
                dve.wait_ge(acc_full, g * NC if ic == 1 else g * NC + 1)
                V.tensor_copy(pv_sb[:, :], ps[:, 0, :]).then_inc(acc_free, 1)

            for t in PRE:
                aux(-1, t, 0)
            V.memset(ps[:, 0, :], 1.0).then_inc(acc_one, 1)
            dve.wait_ge(acc_one, 1)

            def body(g, plan, phase):
                for n in range(NSLOT):
                    if n == 0:
                        evac(g, 1)
                    if n == 8:
                        evac(g, 0)
                    for t in plan[n]:
                        aux(g, t, phase)

            LINKS0 = steps[0]
            LINKS = sum({"gu": 1, "oT": 2}.get(t[0], 0) + (2 if t == max0[-1] else 3 if t == max1[-1] else 0) for t in banked(PLAN1))
            with dve.Fori(0, NH) as g:
                base[0], steps[0] = LINKS * g, LINKS0
                body(g, PLAN1, 1)
            assert steps[0] == LINKS0 + LINKS
            base[0] = LINKS * (NH - 1)
            for g in range(NH, NG):
                body(g, PLAN2[g], 2)
            evac(NG, 1)
            for t in END:
                aux(NG, t, 2)

    return nc


_INS = ["x", "wqkvo", "positions", "directions", "log_scales", "log_amplitudes", "strength", "sensitivity",
        "gsa_gate", "gate_w", "gate_b", "w13", "w2", "ws13", "ws2"]


def kernel(**inputs):
    import numpy as np
    import concourse.bacc as bacc
    from concourse import mybir as mb
    from concourse.bass_utils import run_bass_kernel_spmd as run

    def a(name):
        return np.asarray(inputs[name])

    def c(v):
        return np.ascontiguousarray(v)

    x = a("L0_attn_hidden_states")
    w = [a("L0_attn_" + n) for n in ("Wq", "Wk", "Wv", "Wo")]
    W1, W3, W2 = a("L0_ffn_W1"), a("L0_ffn_W3"), a("L0_ffn_W2")
    laid = {
        "x": x.reshape(x.shape[1], x.shape[2]),
        "wqkvo": np.stack([m.T for m in w]),
        "positions": a("L0_attn_splat_positions").reshape(128, 16),
        "directions": a("L0_attn_splat_directions").reshape(128, 16),
        "log_scales": a("L0_attn_splat_log_scales").reshape(128, 1),
        "log_amplitudes": a("L0_attn_splat_log_amplitudes").reshape(128, 1),
        "strength": a("L0_attn_directional_strength").reshape(1, 1),
        "sensitivity": a("L0_attn_position_sensitivity").reshape(1, 1),
        "gsa_gate": a("L0_attn_gsa_strength").reshape(1, 1),
        "gate_w": a("L0_ffn_gate_w").T,
        "gate_b": a("L0_ffn_gate_b").reshape(1, -1),
        "w13": np.concatenate([W1.transpose(0, 2, 1), W3.transpose(0, 2, 1)], axis=2),
        "w2": W2.transpose(0, 2, 1),
        "ws13": np.concatenate([a("L0_ffn_Ws1").T, a("L0_ffn_Ws3").T], axis=1),
        "ws2": a("L0_ffn_Ws2").T,
    }
    nc = bacc.Bacc("TRN2", target_bir_lowering=False, num_devices=1)
    arrays, args = {}, []
    for name in _INS:
        v = c(laid[name])
        arrays[f"in_{name}_dram"] = v
        args.append(nc.dram_tensor(f"in_{name}_dram", v.shape, mb.dt.from_np(v.dtype), kind="ExternalInput").ap())
    out = nc.dram_tensor("out_dram", (x.shape[1], x.shape[2]), mb.dt.from_np(x.dtype), kind="ExternalOutput").ap()
    bass_splat_attention_moe_layer(nc, *args, out)
    r = run(nc, [arrays], core_ids=[0])
    return r.results[0]["out_dram"].reshape(x.shape)
```
